# Optimizing a Trainium2 kernel written in Bass

```python
import numpy as np
import jax
import jax.numpy as jnp

def _softmax(x, axis=-1):
    return jax.nn.softmax(x, axis=axis)

def _gelu(x):
    return jax.nn.gelu(x, approximate=True)

def _silu(x):
    return jax.nn.silu(x)

def _sigmoid(x):
    return jax.nn.sigmoid(x)

def _layernorm(x, axis=-1, eps=1e-05):
    m = jnp.mean(x, axis=axis, keepdims=True)
    v = jnp.var(x, axis=axis, keepdims=True)
    return (x - m) / jnp.sqrt(v + eps)

def _scatter_add(tgt, idx, src, axis=0):
    return tgt.at[idx].add(src)

def _segment_sum(src, seg, n):
    return jax.ops.segment_sum(src, seg, n)
kernel_name = 'mk_adj_ffn_d1_adj_r2_4711d5'

def setup_inputs(seed: int=0):
    np.random.seed(seed)
    _w = jnp.asarray

    def _rec_inputs():
        import jax
        import jax.numpy as jnp
        _gk = jax.random.key(seed)
        x = -8.015e-05 + 0.9999 * jax.random.normal(jax.random.fold_in(_gk, 1), (8, 1024, 128), jnp.float32)
        _a = jax.random.bernoulli(jax.random.fold_in(_gk, 2), 0.00390625, (8, 1024, 1024))
        _a = jnp.logical_or(_a, jnp.swapaxes(_a, -1, -2))
        _a = jnp.logical_or(_a, jnp.eye(1024, dtype=bool))
        _af = _a.astype(jnp.float32)
        _af = _af * jax.random.uniform(jax.random.fold_in(_gk, 3), (8, 1024, 1024), jnp.float32, 0.05, 0.999837)
        adj = _af
        return (x, adj)
    x, adj = _rec_inputs()

    def _L0_gnn_setup():
        import jax, jax.numpy as jnp
        import numpy as np
        GROUPS = [list(range(25)), [0, 1, 2, 3, 4, 5, 6, 7, 8], [0, 9, 10, 11, 12, 13, 14], [6, 7, 8, 12, 13, 14], [3, 4, 5, 9, 10, 11]]
        B, N, D_IN, D_HID = (4096, 25, 128, 256)

        def _graph_conv(x, adj, W, b):
            n = adj.shape[-1]
            A = adj + jnp.eye(n, dtype=adj.dtype)
            deg = jnp.sum(A, axis=-1)
            deg_safe = jnp.where(deg == 0, 1.0, deg)
            dinv = jnp.where(deg == 0, 0.0, deg_safe ** (-0.5))
            norm_adj = dinv[:, :, None] * A * dinv[:, None, :]
            support = jnp.einsum('bnd,de->bne', x, W)
            out = jnp.einsum('bnm,bme->bne', norm_adj, support) + b
            return jax.nn.relu(out)
        key = jax.random.key(seed)
        ks = jax.random.split(key, 7)
        s1 = float(np.sqrt(6.0 / (D_IN + D_HID)))
        s2 = float(np.sqrt(6.0 / (D_HID + D_IN)))
        return {'x': jax.random.normal(ks[0], (B, N, D_IN), dtype=jnp.float32), 'adj': jax.random.uniform(ks[1], (B, N, N), dtype=jnp.float32), 'W1': jax.random.uniform(ks[2], (5, D_IN, D_HID), jnp.float32, -s1, s1), 'b1': jnp.zeros((5, D_HID), dtype=jnp.float32), 'W2': jax.random.uniform(ks[3], (5, D_HID, D_IN), jnp.float32, -s2, s2), 'b2': jnp.zeros((5, D_IN), dtype=jnp.float32), 'fusion_w': jnp.ones((5,), dtype=jnp.float32)}
    _L0_gnn_all = _L0_gnn_setup()
    _L0_gnn_in = {k: v for k, v in _L0_gnn_all.items() if k in ('W1', 'b1', 'W2', 'b2', 'fusion_w')}
    del _L0_gnn_all

    def _L0_ffn_setup():
        import jax, jax.numpy as jnp
        import numpy as np
        TOP_K = 2
        LN_EPS = 1e-05
        key = jax.random.key(seed)
        ks = jax.random.split(key, 8)
        B, S, D, E, H = (16, 512, 128, 8, 512)
        x = jax.random.normal(ks[0], (B, S, D), dtype=jnp.float32)
        Wr = jax.random.normal(ks[1], (D, E), dtype=jnp.float32) * 0.1
        br = jnp.zeros((E,), dtype=jnp.float32)
        ln_g = jnp.ones((E, D), dtype=jnp.float32)
        ln_b = jnp.zeros((E, D), dtype=jnp.float32)
        W1 = jax.random.normal(ks[2], (E, D, H), dtype=jnp.float32) * (1.0 / np.sqrt(D))
        b1 = jnp.zeros((E, H), dtype=jnp.float32)
        W2 = jax.random.normal(ks[3], (E, H, D), dtype=jnp.float32) * (1.0 / np.sqrt(H))
        b2 = jnp.zeros((E, D), dtype=jnp.float32)
        return {'x': x, 'Wr': Wr, 'br': br, 'ln_g': ln_g, 'ln_b': ln_b, 'W1': W1, 'b1': b1, 'W2': W2, 'b2': b2}
    _L0_ffn_all = _L0_ffn_setup()
    _L0_ffn_in = {k: v for k, v in _L0_ffn_all.items() if k in ('Wr', 'br', 'ln_g', 'ln_b', 'W1', 'b1', 'W2', 'b2')}
    del _L0_ffn_all
    return {'x': x, 'adj': adj, 'L0_gnn_W1': _L0_gnn_in['W1'], 'L0_gnn_b1': _L0_gnn_in['b1'], 'L0_gnn_W2': _L0_gnn_in['W2'], 'L0_gnn_b2': _L0_gnn_in['b2'], 'L0_gnn_fusion_w': _L0_gnn_in['fusion_w'], 'L0_ffn_Wr': _L0_ffn_in['Wr'], 'L0_ffn_br': _L0_ffn_in['br'], 'L0_ffn_ln_g': _L0_ffn_in['ln_g'], 'L0_ffn_ln_b': _L0_ffn_in['ln_b'], 'L0_ffn_W1': _L0_ffn_in['W1'], 'L0_ffn_b1': _L0_ffn_in['b1'], 'L0_ffn_W2': _L0_ffn_in['W2'], 'L0_ffn_b2': _L0_ffn_in['b2']}

def reference(x, adj, L0_gnn_W1, L0_gnn_b1, L0_gnn_W2, L0_gnn_b2, L0_gnn_fusion_w, L0_ffn_Wr, L0_ffn_br, L0_ffn_ln_g, L0_ffn_ln_b, L0_ffn_W1, L0_ffn_b1, L0_ffn_W2, L0_ffn_b2):
    import jax
    import jax.numpy as jnp

    def _L0_gnn_ref(x, adj, W1, b1, W2, b2, fusion_w):
        import jax, jax.numpy as jnp
        import numpy as np
        GROUPS = [list(range(25)), [0, 1, 2, 3, 4, 5, 6, 7, 8], [0, 9, 10, 11, 12, 13, 14], [6, 7, 8, 12, 13, 14], [3, 4, 5, 9, 10, 11]]
        B, N, D_IN, D_HID = (4096, 25, 128, 256)

        def _graph_conv(x, adj, W, b):
            n = adj.shape[-1]
            A = adj + jnp.eye(n, dtype=adj.dtype)
            deg = jnp.sum(A, axis=-1)
            deg_safe = jnp.where(deg == 0, 1.0, deg)
            dinv = jnp.where(deg == 0, 0.0, deg_safe ** (-0.5))
            norm_adj = dinv[:, :, None] * A * dinv[:, None, :]
            support = jnp.einsum('bnd,de->bne', x, W)
            out = jnp.einsum('bnm,bme->bne', norm_adj, support) + b
            return jax.nn.relu(out)
        norm_w = jax.nn.softmax(fusion_w)
        fused = jnp.zeros_like(x)
        for g, idx_list in enumerate(GROUPS):
            idx = jnp.asarray(idx_list)
            x_g = x[:, idx, :]
            adj_g = adj[:, idx][:, :, idx]
            h = _graph_conv(x_g, adj_g, W1[g], b1[g])
            out_g = _graph_conv(h, adj_g, W2[g], b2[g])
            fused = fused.at[:, idx, :].add(norm_w[g] * out_g)
        return fused

    def _L0_ffn_ref(x, Wr, br, ln_g, ln_b, W1, b1, W2, b2):
        import jax, jax.numpy as jnp
        import numpy as np
        TOP_K = 2
        LN_EPS = 1e-05
        B, S, D = x.shape
        N = B * S
        xt = x.reshape(N, D)
        logits = xt @ Wr + br
        probs = jax.nn.softmax(logits, axis=-1)
        top_p, top_idx = jax.lax.top_k(probs, TOP_K)
        weights = top_p / top_p.sum(axis=-1, keepdims=True)
        mu = xt.mean(axis=-1, keepdims=True)
        var = ((xt - mu) ** 2).mean(axis=-1, keepdims=True)
        xn = (xt - mu) * jax.lax.rsqrt(var + LN_EPS)
        xe = xn[None, :, :] * ln_g[:, None, :] + ln_b[:, None, :]
        h = jax.nn.gelu(jnp.einsum('end,edh->enh', xe, W1) + b1[:, None, :], approximate=False)
        y = jnp.einsum('enh,ehd->end', h, W2) + b2[:, None, :]
        y_tok = jnp.transpose(y, (1, 0, 2))
        sel = jnp.take_along_axis(y_tok, top_idx[:, :, None], axis=1)
        out = (weights[:, :, None] * sel).sum(axis=1)
        return out.reshape(B, S, D)
    x = x + _L0_gnn_ref(_layernorm(x, axis=-1), adj, L0_gnn_W1, L0_gnn_b1, L0_gnn_W2, L0_gnn_b2, L0_gnn_fusion_w)
    x = x + _L0_ffn_ref(_layernorm(x, axis=-1), L0_ffn_Wr, L0_ffn_br, L0_ffn_ln_g, L0_ffn_ln_b, L0_ffn_W1, L0_ffn_b1, L0_ffn_W2, L0_ffn_b2)
    return x

_drawn_inputs = setup_inputs


def setup_inputs(seed=0):
    import zlib

    import numpy as np

    out = dict(_drawn_inputs(seed))
    spreads = {'L0_gnn_b1': (0.0, 2.0),
     'L0_gnn_b2': (0.0, 0.8),
     'L0_gnn_fusion_w': (1.0, 0.6),
     'L0_ffn_br': (0.0, 0.1),
     'L0_ffn_ln_g': (1.0, 0.2),
     'L0_ffn_ln_b': (0.0, 0.1),
     'L0_ffn_b1': (0.0, 0.1),
     'L0_ffn_b2': (0.0, 0.1)}
    factors = {'adj': 32.711, 'L0_gnn_W1': 2.757}
    for name, (base, spread) in spreads.items():
        noise = np.random.default_rng([zlib.crc32(name.encode()), seed]).standard_normal(out[name].shape)
        drawn = base * np.exp(spread * noise) if base else spread * noise
        out[name] = jnp.asarray(drawn.astype(out[name].dtype))
    for name, factor in factors.items():
        out[name] = (out[name] * factor).astype(out[name].dtype)
    return out
```

```python
from contextlib import ExitStack

import numpy as np

import concourse.bass as bass
import concourse.mybir as mybir

ALU = mybir.AluOpType
ACT = mybir.ActivationFunctionType
F32 = mybir.dt.float32
F16 = mybir.dt.float16
BF16 = mybir.dt.bfloat16
I32 = mybir.dt.int32
U32 = mybir.dt.uint32
AX_X = mybir.AxisListType.X
RMAX = bass.bass_isa.ReduceOp.max

P = 128
GROUPS = [list(range(25)), [0, 1, 2, 3, 4, 5, 6, 7, 8], [0, 9, 10, 11, 12, 13, 14],
          [6, 7, 8, 12, 13, 14], [3, 4, 5, 9, 10, 11]]
NODES = 25
SLOT = 32
EPS = 1e-5

W_PARTS, W_RES, W_ID, W_GATE, W_ROW = 0, 128, 256, 257, 260
UNROLL = 4


def group_tables():
    member = np.zeros((P, len(GROUPS)), np.float32)
    for g, nodes in enumerate(GROUPS):
        for j in range(P // SLOT):
            member[[SLOT * j + n for n in nodes], g] = 1.0
    both = member[:, :, None] * member.T[None, :, :]
    return np.ascontiguousarray(both.reshape(P, -1)), member


def blocks_bound(tokens, experts):
    pairs = experts * (experts - 1) // 2
    bound = (tokens + pairs * (P - 1)) // P
    return -(-bound // UNROLL) * UNROLL


def build(nc, x, adj, gW1, gb1, gW2, gb2, fusion, Wr, br, ln_g, ln_b, W1, b1, W2, b2,
          both_in, member_in, out):
    B, S, D = x.shape
    E, _, H = W1.shape
    NG, _, GH = gW1.shape
    assert D == P
    T = B * S // P
    TB = S // P
    HC = H // P
    GC = GH // P
    NCLS = E * E
    NB = blocks_bound(B * S, E)
    NIT = NB // UNROLL
    HALF = B * SLOT // P
    BPH = P // SLOT
    K = NG * HALF
    SX = 11

    x_tok = x.rearrange("b (t p) d -> p (b t) d", p=P)
    out_rows = out.rearrange("b s d -> (b s) d")
    pool = nc.dram_tensor("pool", [NB * P, W_ROW], F32, kind="Internal").ap()

    with ExitStack() as ctx:
        def sb(name, shape, dt=F32):
            return ctx.enter_context(nc.sbuf_tensor(name, shape, dt))

        def sem(name):
            return ctx.enter_context(nc.semaphore(name))

        bank = [ctx.enter_context(nc.psum_tensor(f"bank{i}", [P, 512], F32)) for i in range(8)]

        rows = sb("rows", [P, T, W_ROW])
        res = rows[:, :, W_RES:W_RES + D]
        parts = rows[:, :, W_PARTS:W_PARTS + D].bitcast(F16)
        hi_part, lo_part = parts[:, :, 0:D], parts[:, :, D:2 * D]
        ids = rows[:, :, W_ID:W_ID + 1].bitcast(I32)
        gate = rows[:, :, W_GATE:W_GATE + 2]
        xt = sb("xt", [P, T, D])
        fill = sb("fill", [P, W_ROW])
        stats = sb("stats", [P, T, 6])
        mean = sb("mean", [P, T])
        rstd = sb("rstd", [P, T])
        var = sb("var", [P, T])
        tmp = sb("tmp", [P, T])

        ident = sb("ident", [P, P])
        ident16 = sb("ident16", [P, P], F16)
        ones = sb("ones", [P, P])
        ones16 = sb("ones16", [P, P], BF16)
        tri = sb("tri", [P, P], BF16)
        iota_c = sb("iota_c", [P, NCLS])
        iota_p = sb("iota_p", [P, 1])
        delta = sb("delta", [P, 16])

        stage = sb("stage", [P, P])
        cols = sb("cols", [P, 64])
        w_f = sb("w_f", [P, E * H])
        w1p = sb("w1p", [P, 2, E * H], F16)
        w2p = sb("w2p", [P, 2, E * H], F16)
        b1T = sb("b1T", [P, E * HC])
        wmax = sb("wmax", [P, 4])
        wtop = sb("wtop", [P, 4])
        pow2 = sb("pow2", [P, 4])
        scl = sb("scl", [P, 8])
        wr_sb = sb("wr_sb", [P, E])
        br_b = sb("br_b", [P, E])
        b2rep = sb("b2rep", [P, D])

        gx = sb("gx", [P, HALF, D])
        gsmall = sb("gsmall", [P, 64])
        gmean, gvar, grstd, gtmp = (gsmall[:, 2 * i:2 * i + 2] for i in range(4))
        gdeg, gdinv, gzero, gsafe = (gsmall[:, 10 + 10 * i:20 + 10 * i] for i in range(4))
        gstats = sb("gstats", [P, HALF, 6])
        fus = sb("fus", [P, NG])
        member = sb("member", [P, NG])
        gsc = sb("gsc", [P, 4])
        gb2r = sb("gb2r", [1, NG * D])
        gout = sb("gout", [P, HALF, D])
        gadd = sb("gadd", [NODES, B, D])
        xt_flat = xt[:, :, :].rearrange("p t d -> p (t d)")
        a0 = 0

        def take(n):
            nonlocal a0
            a0 += n
            return xt_flat[:, a0 - n:a0]

        gW1s = take(NG * GH)
        gW2s = take(NG * GC * D)
        gboth = take(NG * P)
        gA = take(K * P)
        gNT = take(K * P)
        xaT = w_f[:, 0:K * P]
        gS2 = w_f[:, K * P:2 * K * P]
        assert a0 <= T * D and 2 * K * P <= E * H
        h1T = w1p[:, :, :].rearrange("p a n -> p (a n)").bitcast(F32)[:, 0:NG * GC * HALF * P]
        gZ = w2p[:, 0, 0:2 * HALF * P].bitcast(F32)
        gF = w2p[:, 1, 0:2 * K * P].bitcast(F32)

        logit = sb("logit", [P, T, E])
        big = sb("big", [P, T, E])
        oh1 = sb("oh1", [P, T, E])
        oh2 = sb("oh2", [P, T, E])
        rt = sb("rt", [P, 12, T])
        top1, top2, i1, i2, ex2, g1, g2, sel, cls, rank, ia, ib = (rt[:, i, :] for i in range(12))
        onehot = sb("onehot", [P, T, NCLS], BF16)
        before = sb("before", [P, T + 1, NCLS], BF16)
        place = xt_flat[:, 0:T * NCLS].rearrange("p (t c) -> p t c", c=NCLS)
        pos = sb("pos", [P, T], U32)
        cnt = sb("cnt", [P, 8, NCLS])
        cnt_i = sb("cnt_i", [P, NCLS], I32)
        base16 = sb("base16", [P, NCLS], BF16)
        bcls = sb("bcls", [P, 2])
        wg = sb("wg", [P, 2 * UNROLL])
        cmp = sb("cmp", [P, NCLS])
        blk_i = sb("blk_i", [1, 3, P], I32)
        blk_e = sb("blk_e", [1, 2 * P], I32)
        GT = sb("GT", [P, P])
        b2x = xt_flat[:, T * NCLS:T * NCLS + 16 * D].rearrange("p (t d) -> p t d", d=D)

        blk = xt_flat[:, 0:UNROLL * W_ROW].rearrange("p (k w) -> p k w", w=W_ROW)
        off = [UNROLL * W_ROW]

        def carve(n):
            off[0] += n
            return xt_flat[:, off[0] - n:off[0]]

        bT = carve(2 * D).bitcast(F16).rearrange("p (k w) -> p k w", k=2)
        hf = carve(UNROLL * H).rearrange("p (k h) -> p k h", k=UNROLL)
        hp = carve(UNROLL * H).bitcast(F16).rearrange("p (k a h) -> p k a h", k=UNROLL, a=2)
        ob = carve(UNROLL * D).rearrange("p (k d) -> p k d", k=UNROLL)
        assert off[0] <= T * D

        x_in = [sem(f"x_in{i}") for i in range(8)]
        gx_in = sem("gx_in")
        gadj_in = sem("gadj_in")
        gw_in = sem("gw_in")
        small_in = sem("small_in")
        w1_in = sem("w1_in")
        w2_in = sem("w2_in")
        b2_in = sem("b2_in")
        gadd_in = sem("gadd_in")
        h_hi = sem("h_hi")
        wg_ready = sem("wg_ready")
        storing = sem("storing")
        pool_filled = sem("pool_filled")
        consts = sem("consts")
        zeroed = sem("zeroed")
        v = sem("v")
        dve_stage = sem("dve_stage")
        need_sqrt = sem("need_sqrt")
        sqrt_done = sem("sqrt_done")
        fus_exp = sem("fus_exp")
        gA_ready = sem("gA_ready")
        gT_done = sem("gT_done")
        gNT_ready = sem("gNT_ready")
        xa_done = sem("xa_done")
        xaT_ready = sem("xaT_ready")
        h1_done = sem("h1_done")
        h1_act = sem("h1_act")
        s2_done = sem("s2_done")
        s2_ready = sem("s2_ready")
        go_done = sem("go_done")
        gout_ready = sem("gout_ready")
        stage_T = sem("stage_T")
        cols_ready = sem("cols_ready")
        bias_done = sem("bias_done")
        wmax_ready = sem("wmax_ready")
        wtop_ready = sem("wtop_ready")
        w2_free = sem("w2_free")
        xt_ready = sem("xt_ready")
        xtT_done = sem("xtT_done")
        xtT_ready = sem("xtT_ready")
        logit_done = sem("logit_done")
        logit_read = sem("logit_read")
        need_exp = sem("need_exp")
        exp_done = sem("exp_done")
        gates_ready = sem("gates_ready")
        GT_done = sem("GT_done")
        GT_ready = sem("GT_ready")
        b2x_ready = sem("b2x_ready")
        bias_sum = sem("bias_sum")
        bias_added = sem("bias_added")
        counts_ready = sem("counts_ready")
        total_done = sem("total_done")
        base_ready = sem("base_ready")
        rank_done = sem("rank_done")
        pos_ready = sem("pos_ready")
        sent = sem("sent")
        bcls_ready = sem("bcls_ready")
        bcls_T = sem("bcls_T")
        table_ready = sem("table_ready")
        weights_ready = sem("weights_ready")
        blk_in = [sem(f"blk_in{k}") for k in range(UNROLL)]
        blk_T = sem("blk_T")
        bT_ready = sem("bT_ready")
        up_done = sem("up_done")
        gelu_done = sem("gelu_done")
        split_done = sem("split_done")
        down_done = sem("down_done")
        mixed = sem("mixed")
        stored = [sem(f"stored{k}") for k in range(UNROLL)]

        n_small = 0
        block = ctx.enter_context(nc.Block())

        def rt_buf(q):
            return w1p[:, 0, :].bitcast(F32)[:, (q % 2) * 512:(q % 2) * 512 + 512]

        def unit_loop(eng, step):
            for k in range(UNROLL):
                step(k, k, None)
            with eng.Fori(1, NIT - 1) as it:
                for k in range(UNROLL):
                    step(it * UNROLL + k, k, it)
            for k in range(UNROLL):
                step((NIT - 1) * UNROLL + k, k, NIT - 1)

        @block.sync
        def _(sp):
            sp.wait_ge(zeroed, 2)
            for b in range(B):
                p0 = SLOT * (b % BPH)
                sp.dma_start(gx[p0:p0 + NODES, b // BPH, :], x[b, 0:NODES, :]).then_inc(gx_in, 16)
            for b in range(B):
                p0 = SLOT * (b % BPH)
                c0 = (b // BPH) * P + p0
                sp.dma_start(gZ[p0:p0 + NODES, c0:c0 + NODES], adj[b, 0:NODES, 0:NODES]).then_inc(gadj_in, 16)
            for b in range(B):
                sp.dma_start(res[:, TB * b:TB * b + TB, :], x_tok[:, TB * b:TB * b + TB, :]).then_inc(x_in[b], 16)
            for i in range(P // E):
                sp.dma_start(b2rep[i * E:(i + 1) * E, :], b2).then_inc(b2_in, 16)
            sp.wait_ge(zeroed, 4)
            sp.dma_start(pool.rearrange("(j p) w -> p j w", p=P),
                         fill[:, :].rearrange("p (o w) -> p o w", o=1).to_broadcast([P, NB, W_ROW])
                         ).then_inc(pool_filled, 16)
            sp.wait_ge(gout_ready, 1)
            for b in range(B):
                p0 = SLOT * (b % BPH)
                sp.dma_start(gadd[:, b, :], gout[p0:p0 + NODES, b // BPH, :]).then_inc(gadd_in, 16)
            sp.wait_ge(sent, 16 * T)

            def load(j, k, it):
                row = j * P if it is None or isinstance(it, int) else sp.snap(j * P)
                if it is not None:
                    sp.wait_ge(stored[k], 16 * it)
                sp.dma_start(blk[:, k, :], pool[bass.ds(row, P), :]).then_inc(blk_in[k], 16)

            unit_loop(sp, load)
            for k in range(UNROLL):
                sp.wait_ge(stored[k], 16 * NIT)

        @block.gpsimd
        def _(po):
            po.memset(gx[:, :, :], 0.0).then_inc(zeroed, 1)
            po.memset(gZ, 0.0).then_inc(zeroed, 1)
            po.memset(fill[:, :], 0.0).then_inc(zeroed, 1)
            po.wait_ge(zeroed, 3)
            po.iota(fill[:, W_ID:W_ID + 1].bitcast(I32), [[0, 1]], base=1 << 20, channel_multiplier=0
                    ).then_inc(zeroed, 1)
            po.memset(ident[:, :], 0.0).then_inc(consts, 1)
            po.memset(ident16[:, :], 0.0).then_inc(consts, 1)
            po.memset(tri[:, :], 1.0).then_inc(consts, 1)
            po.memset(delta[:, :], 1.0).then_inc(consts, 1)
            po.memset(ones[:, :], 1.0).then_inc(consts, 1)
            po.memset(ones16[:, :], 1.0).then_inc(consts, 1)
            po.memset(before[:, 0, :], 0.0).then_inc(consts, 1)
            po.iota(iota_c[:, :], [[1, NCLS]], base=0, channel_multiplier=0,
                    allow_small_or_imprecise_dtypes=True).then_inc(consts, 1)
            po.iota(iota_p[:, :], [[0, 1]], base=0, channel_multiplier=1,
                    allow_small_or_imprecise_dtypes=True).then_inc(consts, 1)
            po.wait_ge(consts, 9)
            for m in (ident, ident16):
                po.affine_select(out=m[:, :], in_=m[:, :], compare_op=ALU.not_equal, fill=1.0, base=0,
                                 pattern=[[-1, P]], channel_multiplier=1).then_inc(consts, 1)
            po.affine_select(out=tri[:, :], in_=tri[:, :], compare_op=ALU.is_gt, fill=0.0, base=0,
                             pattern=[[1, P]], channel_multiplier=-1).then_inc(consts, 1)
            po.affine_select(out=delta[:, :], in_=delta[:, :], compare_op=ALU.is_ge, fill=0.0, base=0,
                             pattern=[[-E, 16]], channel_multiplier=1).then_inc(consts, 1)
            po.wait_ge(consts, 13)
            po.affine_select(out=delta[:, :], in_=delta[:, :], compare_op=ALU.is_ge, fill=0.0, base=E - 1,
                             pattern=[[E, 16]], channel_multiplier=-1).then_inc(consts, 1)
            po.memset(rows[:, :, W_ROW - 1:W_ROW], 0.0).then_inc(consts, 1)
            po.iota(ids, [[P, T]], base=0, channel_multiplier=1).then_inc(consts, 1)
            po.wait_ge(pool_filled, 16)
            po.wait_ge(pos_ready, 1)
            po.wait_ge(consts, 16)
            for t in range(T):
                if t % 4 == 0:
                    po.wait_ge(bias_added, t // 4 + 1)
                po.indirect_dma_start(pool, bass.IndirectOffsetOnAxis(ap=pos[:, t:t + 1], axis=0),
                                      rows[:, t, :], None, bounds_check=NB * P - 1,
                                      oob_is_err=False).then_inc(sent, 16)

            for n in range(2):
                po.wait_ge(wmax_ready, n + 1)
                po.partition_all_reduce(wtop[:, :], wmax[:, :], P, RMAX).then_inc(wtop_ready, 1)

            def store(j, k, it):
                po.wait_ge(mixed, 2 * j + 2)
                po.sem_inc(storing, 1)
                po.indirect_dma_start(out_rows, bass.IndirectOffsetOnAxis(
                    ap=blk[:, k, W_ID:W_ID + 1].bitcast(U32), axis=0), ob[:, k, :], None,
                    bounds_check=B * S - 1, oob_is_err=False).then_inc(stored[k], 16)

            unit_loop(po, store)
            for k in range(UNROLL):
                po.wait_ge(stored[k], 16 * NIT)

        @block.scalar
        def _(act):
            act.dma_start(gboth, both_in).then_inc(gw_in, 16)
            act.dma_start(member[:, :], member_in).then_inc(gw_in, 16)
            act.dma_start(gW1s.rearrange("p (g h) -> p g h", g=NG), gW1.rearrange("g d h -> d g h")).then_inc(gw_in, 16)
            for g in range(NG):
                act.dma_start(gW2s[:, g * GC * D:(g + 1) * GC * D].rearrange("p (c d) -> p c d", c=GC),
                              gW2[g].rearrange("(c p) d -> p c d", p=P)).then_inc(gw_in, 16)
            act.dma_start(gb2r[:, :], gb2.rearrange("(o g) d -> o (g d)", o=1)).then_inc(gw_in, 16)
            act.dma_start(fus[:, :], fusion.rearrange("(o g) -> o g", o=1).to_broadcast([P, NG])).then_inc(gw_in, 16)
            act.wait_ge(dve_stage, 1)
            act.dma_start(stage[0:E * HC, :], b1.rearrange("e (c h) -> (e c) h", h=P)).then_inc(small_in, 16)
            act.dma_start(stage[32:32 + E, :], ln_g).then_inc(small_in, 16)
            act.dma_start(stage[40:40 + E, :], ln_b).then_inc(small_in, 16)
            act.dma_start(stage[48:48 + NG * GC, :], gb1.rearrange("g (c h) -> (g c) h", h=P)).then_inc(small_in, 16)
            act.dma_start(wr_sb[:, :], Wr).then_inc(small_in, 16)
            act.dma_start(br_b[:, :], br.rearrange("(o e) -> o e", o=1).to_broadcast([P, E])).then_inc(small_in, 16)
            act.wait_ge(need_exp, 1)
            act.activation(fus[:, :], fus[:, :], ACT.Exp, bias=gsc[:, 0:1], accum_out=gsc[:, 1:2]).then_inc(fus_exp, 1)
            act.wait_ge(need_sqrt, 1)
            act.activation(grstd, gtmp, ACT.Sqrt).then_inc(sqrt_done, 1)
            act.wait_ge(need_sqrt, 2)
            act.activation(gdinv, gsafe, ACT.Sqrt).then_inc(sqrt_done, 1)
            for n in range(NG * GC):
                if n % 2 == 0:
                    act.wait_ge(h1_done, n // 2 + 1)
                if n == 0:
                    act.wait_ge(cols_ready, 1)
                act.activation(h1T[:, n * HALF * P:(n + 1) * HALF * P], bank[n // 2][:, (n % 2) * 256:(n % 2) * 256 + HALF * P],
                               ACT.Relu, bias=cols[:, 48 + n:49 + n]).then_inc(h1_act, 1)
            act.wait_ge(go_done, 3)
            act.wait_ge(gout_ready, 1)
            act.dma_start(w_f[:, :].rearrange("p (e h) -> p e h", e=E), W1.rearrange("e d h -> d e h")).then_inc(w1_in, 16)
            for n in range(2):
                act.wait_ge(need_sqrt, 3 + n)
                act.activation(rstd[:, :], tmp[:, :], ACT.Sqrt).then_inc(sqrt_done, 1)
                if n == 0:
                    for q in range(T // 4):
                        act.wait_ge(xtT_done, q + 1)
                        if q >= 2:
                            act.wait_ge(logit_done, 4 * (q - 1))
                        act.activation(rt_buf(q), bank[q % 2][:, :], ACT.Copy).then_inc(xtT_ready, 1)
            act.wait_ge(need_exp, 2)
            act.activation(ex2, ex2, ACT.Exp).then_inc(exp_done, 1)
            act.wait_ge(w2_free, 1)
            for e in range(E):
                act.dma_start(w_f[:, e * H:(e + 1) * H].rearrange("p (c d) -> p c d", c=HC),
                              W2[e].rearrange("(c p) d -> p c d", p=P)).then_inc(w2_in, 16)
            act.wait_ge(weights_ready, 1)
            act.wait_ge(table_ready, 1)

            def gelus(j, k, it):
                for s in range(2):
                    u, n = 2 * j + s, (2 * k + s) % 4
                    e = act.value_load(blk_e[0:1, bass.ds(u, 1)], min_val=0, max_val=E - 1)
                    first = act.snap(e * HC)
                    act.wait_ge(up_done, u + 1)
                    if it is not None or k >= 2:
                        act.wait_ge(split_done, u - 3)
                    for c in range(HC):
                        ins = act.activation(hf[:, n, c * P:(c + 1) * P], bank[n][:, c * P:(c + 1) * P], ACT.Gelu,
                                             bias=b1T[:, bass.ds(first + c, 1)], scale=scl[:, 2:3])
                    ins.then_inc(gelu_done, 1)

            unit_loop(act, gelus)

        @block.vector
        def _(ve):
            made = [0]

            def after(ins):
                made[0] += 1
                ins.then_inc(v, 1)
                ve.wait_ge(v, made[0])

            told = {}

            def tell(ins, s):
                told[s.name] = told.get(s.name, 0) + 1
                ins.then_inc(s, 1)
                ve.wait_ge(s, told[s.name])

            sqrts = [0]

            def inverse_root(out_, var_, tmp_, newton):
                after(ve.tensor_scalar(var_, var_, EPS, None, ALU.add))
                tell(ve.reciprocal(tmp_, var_), need_sqrt)
                sqrts[0] += 1
                ve.wait_ge(sqrt_done, sqrts[0])
                newton_step(out_, var_, tmp_)

            def newton_step(out_, y, tmp_):
                after(ve.tensor_tensor(tmp_, out_, out_, ALU.mult))
                after(ve.tensor_tensor(tmp_, tmp_, y, ALU.mult))
                after(ve.tensor_scalar(tmp_, tmp_, -0.5, 1.5, ALU.mult, ALU.add))
                after(ve.tensor_tensor(out_, out_, tmp_, ALU.mult))

            def moments(st, mean_, var_, tmp_):
                n = D // 2
                after(ve.tensor_tensor(tmp_, st[:, :, 1], st[:, :, 4], ALU.subtract))
                after(ve.tensor_tensor(mean_, st[:, :, 1], st[:, :, 4], ALU.add))
                after(ve.tensor_scalar(mean_, mean_, 0.5, None, ALU.mult))
                after(ve.tensor_tensor(tmp_, tmp_, tmp_, ALU.mult))
                after(ve.tensor_tensor(var_, st[:, :, 2], st[:, :, 5], ALU.add))
                after(ve.tensor_scalar(var_, var_, 1.0 / (2 * n), None, ALU.mult))
                after(ve.scalar_tensor_tensor(var_, tmp_, 0.25, var_, ALU.mult, ALU.add))

            tell(ve.memset(stage[:, :], 0.0), dve_stage)

            ve.wait_ge(gw_in, 16 * (5 + NG))
            ve.wait_ge(small_in, 16 * 6)
            after(ve.tensor_reduce(gsc[:, 0:1], fus[:, :], AX_X, ALU.max))
            tell(ve.tensor_scalar(gsc[:, 0:1], gsc[:, 0:1], -1.0, None, ALU.mult), need_exp)
            ve.wait_ge(gx_in, 16 * B)
            for h in range(HALF):
                after(ve.bn_stats(gstats[:, h, :], gx[:, h, :]))
            moments(gstats[:, :, :], gmean, gvar, gtmp)
            inverse_root(grstd, gvar, gtmp, True)
            for h in range(HALF):
                after(ve.tensor_scalar(gx[:, h, :], gx[:, h, :], gmean[:, h:h + 1], grstd[:, h:h + 1],
                                       ALU.subtract, ALU.mult))
            ve.wait_ge(gadj_in, 16 * B)
            ve.wait_ge(consts, 11)
            gA4 = gA.rearrange("p (h g m) -> p h g m", h=HALF, g=NG)
            for h in range(HALF):
                after(ve.tensor_tensor(gZ[:, h * P:(h + 1) * P], gZ[:, h * P:(h + 1) * P], ident[:, :], ALU.add))
                after(ve.tensor_tensor(gA4[:, h], gZ[:, h * P:(h + 1) * P].rearrange("p (o m) -> p o m", o=1).to_broadcast([P, NG, P]),
                                       gboth.rearrange("p (g m) -> p g m", g=NG), ALU.mult))
            gA3 = gA.rearrange("p (k m) -> p k m", k=K)
            after(ve.tensor_reduce(gdeg, gA3, AX_X, ALU.add))
            after(ve.tensor_scalar(gzero, gdeg, 0.0, None, ALU.is_equal))
            after(ve.tensor_tensor(gdeg, gdeg, gzero, ALU.add))
            tell(ve.reciprocal(gsafe, gdeg), need_sqrt)
            sqrts[0] += 1
            ve.wait_ge(sqrt_done, sqrts[0])
            newton_step(gdinv, gdeg, gsafe)
            after(ve.tensor_scalar(gzero, gzero, -1.0, 1.0, ALU.mult, ALU.add))
            after(ve.tensor_tensor(gdinv, gdinv, gzero, ALU.mult))

            def spread(a, n):
                return a.rearrange("p (k o) -> p k o", o=1).to_broadcast([P, n, P])

            tell(ve.tensor_tensor(gA3, gA3, spread(gdinv, K), ALU.mult), gA_ready)
            ve.wait_ge(stage_T, 1)
            tell(ve.tensor_copy(cols[:, 0:64], bank[7][:, 0:64]), cols_ready)
            gN3 = gNT.rearrange("p (k m) -> p k m", k=K)
            for q in range(3):
                n = min(4, K - 4 * q)
                ve.wait_ge(gT_done, q + 1)
                tell(ve.tensor_tensor(gN3[:, 4 * q:4 * q + n], bank[q][:, 0:n * P].rearrange("p (k m) -> p k m", k=n),
                                      spread(gdinv[:, 4 * q:4 * q + n], n), ALU.mult), gNT_ready)
            xa4 = xaT.rearrange("p (g h m) -> p g h m", g=NG, h=HALF)
            for h in range(HALF):
                ve.wait_ge(xa_done, h + 1)
                after(ve.tensor_copy(xa4[:, 0:4, h, :], bank[3 + h][:, :].rearrange("p (g m) -> p g m", g=4)))
                tell(ve.tensor_copy(xa4[:, 4, h, :], bank[5 + h][:, 0:P]), xaT_ready)
            for q in range(3):
                n = min(4, K - 4 * q)
                ve.wait_ge(s2_done, q + 1)
                tell(ve.tensor_copy(gS2[:, 4 * q * P:(4 * q + n) * P], bank[5 + q][:, 0:n * P]), s2_ready)
            ve.wait_ge(fus_exp, 1)
            after(ve.reciprocal(gsc[:, 2:3], gsc[:, 1:2]))
            after(ve.scalar_tensor_tensor(fus[:, :], fus[:, :], gsc[:, 2:3], member[:, :], ALU.mult, ALU.mult))
            wk = fus[:, :]
            for q in range(3):
                ve.wait_ge(go_done, q + 1)
                for i in range(min(4, K - 4 * q)):
                    k = 4 * q + i
                    after(ve.tensor_scalar(gF[:, k * P:(k + 1) * P], bank[q][:, i * P:(i + 1) * P], 0.0,
                                           wk[:, k % NG:k % NG + 1], ALU.max, ALU.mult))
            tell(ve.tensor_reduce(gout[:, :, :], gF.rearrange("p (h g d) -> p h d g", h=HALF, g=NG), AX_X, ALU.add),
                 gout_ready)
            ve.wait_ge(gadd_in, 16 * B)
            for b in range(B):
                ve.wait_ge(x_in[b], 16)
            first = res.rearrange("p (b t) d -> p b t d", b=B)[0:NODES, :, 0, :]
            after(ve.tensor_tensor(first, first, gadd[:, :, :], ALU.add))

            for t in range(T):
                ins = ve.bn_stats(stats[:, t, :], res[:, t, :])
            after(ins)
            moments(stats[:, :, :], mean[:, :], var[:, :], tmp[:, :])
            inverse_root(rstd[:, :], var[:, :], tmp[:, :], True)
            for t in range(T):
                ins = ve.tensor_scalar(xt[:, t, :], res[:, t, :], mean[:, t:t + 1], rstd[:, t:t + 1],
                                       ALU.subtract, ALU.mult)
                if t % 4 == 3:
                    tell(ins, xt_ready)
            for t in range(T):
                ins = ve.bn_stats(stats[:, t, :], xt[:, t, :])
            after(ins)
            moments(stats[:, :, :], mean[:, :], var[:, :], tmp[:, :])
            inverse_root(rstd[:, :], var[:, :], tmp[:, :], True)
            after(ve.tensor_scalar(rstd[:, :], rstd[:, :], float(2 ** SX), None, ALU.mult))
            ve.wait_ge(xtT_done, T // 4)
            for t in range(T):
                ins = ve.tensor_scalar(xt[:, t, :], xt[:, t, :], mean[:, t:t + 1], rstd[:, t:t + 1],
                                       ALU.subtract, ALU.mult)
            after(ins)
            after(ve.tensor_copy(hi_part, xt[:, :, :]))
            after(ve.tensor_tensor(lo_part, xt[:, :, :], hi_part, ALU.subtract))

            def over(a):
                return a.rearrange("p (t o) -> p t o", o=1).to_broadcast([P, T, E])

            def along(a):
                return a.rearrange("p (o e) -> p o e", o=1).to_broadcast([P, T, E])

            for q in range(T // 4):
                ve.wait_ge(logit_done, 4 * (q + 1))
            after(ve.tensor_tensor(logit[:, :, :], bank[4][:, :].rearrange("p (t e) -> p t e", e=E), along(br_b[:, :]), ALU.add))
            for top, ix, oh in ((top1, i1, oh1), (top2, i2, oh2)):
                after(ve.tensor_reduce(top, logit[:, :, :], AX_X, ALU.max))
                after(ve.tensor_tensor(big[:, :, :], logit[:, :, :], over(top), ALU.is_equal))
                after(ve.scalar_tensor_tensor(big[:, :, :], big[:, :, :], -float(E), along(iota_c[:, 0:E]), ALU.mult, ALU.add))
                after(ve.tensor_reduce(ix, big[:, :, :], AX_X, ALU.min))
                after(ve.tensor_scalar(ix, ix, float(E), None, ALU.add))
                after(ve.tensor_tensor(oh[:, :, :], over(ix), along(iota_c[:, 0:E]), ALU.is_equal))
                if oh is oh1:
                    after(ve.scalar_tensor_tensor(logit[:, :, :], oh[:, :, :], -3.0e38, logit[:, :, :], ALU.mult, ALU.add))
            tell(ve.tensor_tensor(ex2, top2, top1, ALU.subtract), need_exp)
            after(ve.tensor_tensor(ia, i1, i2, ALU.min))
            after(ve.tensor_tensor(ib, i1, i2, ALU.max))
            after(ve.scalar_tensor_tensor(cls, ia, float(E), ib, ALU.mult, ALU.add))
            after(ve.tensor_tensor(onehot[:, :, :], cls.rearrange("p (t o) -> p t o", o=1).to_broadcast([P, T, NCLS]),
                                   iota_c[:, :].rearrange("p (o c) -> p o c", o=1).to_broadcast([P, T, NCLS]), ALU.is_equal))
            for t in range(T):
                ins = ve.tensor_tensor(before[:, t + 1, :], before[:, t, :], onehot[:, t, :], ALU.add)
                if t < T - 1:
                    after(ins)
                else:
                    tell(ins, counts_ready)
            ve.wait_ge(exp_done, 1)
            after(ve.tensor_scalar(g1, ex2, 1.0, None, ALU.add))
            after(ve.reciprocal(g1, g1))
            after(ve.tensor_tensor(g2, ex2, g1, ALU.mult))
            after(ve.tensor_tensor(oh1[:, :, :], oh1[:, :, :], over(g1), ALU.mult))
            after(ve.tensor_tensor(oh2[:, :, :], oh2[:, :, :], over(g2), ALU.mult))
            tell(ve.tensor_tensor(oh1[:, :, :], oh1[:, :, :], oh2[:, :, :], ALU.add), gates_ready)
            after(ve.tensor_tensor(sel, i1, i2, ALU.is_lt))
            after(ve.tensor_tensor(i1, g1, g2, ALU.subtract))
            after(ve.tensor_tensor(i1, i1, sel, ALU.mult))
            after(ve.tensor_tensor(gate[:, :, 0], g2, i1, ALU.add))
            after(ve.tensor_tensor(gate[:, :, 1], g1, i1, ALU.subtract))

            total, blocks_f, upto, base, one_row = (cnt[:, i, :] for i in range(5))
            ve.wait_ge(total_done, 1)
            after(ve.tensor_scalar(total, bank[5][:, 0:NCLS], float(P - 1), None, ALU.add))
            after(ve.tensor_copy(cnt_i[:, :], total))
            after(ve.tensor_scalar(cnt_i[:, :], cnt_i[:, :], 7, None, ALU.logical_shift_right))
            after(ve.tensor_copy(blocks_f, cnt_i[:, :]))
            after(ve.memset(one_row, 1.0))
            after(ve.tensor_tensor_scan(upto, one_row, blocks_f, 0.0, ALU.mult, ALU.add))
            tell(ve.tensor_tensor(base16[:, :], upto, blocks_f, ALU.subtract), base_ready)
            for q in range(8):
                ve.wait_ge(rank_done, q + 1)
                ins = ve.tensor_tensor(place[:, 8 * q:8 * q + 8, :], bank[q][:, :].rearrange("p (t c) -> p t c", c=NCLS),
                                       onehot[:, 8 * q:8 * q + 8, :], ALU.mult)
            after(ins)
            after(ve.tensor_reduce(rank, place, AX_X, ALU.add))
            tell(ve.tensor_copy(pos[:, :], rank), pos_ready)
            ve.wait_ge(consts, 16)
            ve.wait_ge(b2_in, 16 * (P // E))
            tell(ve.tensor_tensor(b2x, b2rep[:, :].rearrange("p (o d) -> p o d", o=1).to_broadcast([P, 16, D]),
                                   delta[:, :].rearrange("p (t o) -> p t o", o=1).to_broadcast([P, 16, D]), ALU.mult), b2x_ready)
            for r in range(T // 16):
                ve.wait_ge(GT_done, r + 1)
                tell(ve.tensor_copy(GT[:, :], bank[0][:, 0:P]), GT_ready)
                for q in range(4):
                    n = 4 * r + q
                    ve.wait_ge(bias_sum, n + 1)
                    t0 = 4 * n
                    tell(ve.tensor_tensor(res[:, t0:t0 + 4, :], res[:, t0:t0 + 4, :],
                                          bank[1 + q][:, :].rearrange("p (t d) -> p t d", d=D), ALU.add), bias_added)

            after(ve.tensor_scalar(cmp[:, :], upto, iota_p[:, 0:1], None, ALU.is_le))
            after(ve.tensor_reduce(bcls[:, 0:1], cmp[:, :], AX_X, ALU.add))
            tell(ve.tensor_scalar(bcls[:, 0:1], bcls[:, 0:1], float(NCLS - 1), None, ALU.min), bcls_ready)
            ve.wait_ge(bcls_T, 1)
            after(ve.tensor_copy(blk_i[0:1, 0, :], bank[6][0:1, 0:P]))
            pair_e = blk_e[0:1, :].rearrange("o (j s) -> o j s", s=2)
            after(ve.tensor_scalar(pair_e[:, :, 0], blk_i[0:1, 0, :], 3, None, ALU.logical_shift_right))
            tell(ve.tensor_scalar(pair_e[:, :, 1], blk_i[0:1, 0, :], E - 1, None, ALU.bitwise_and), table_ready)

            ve.wait_ge(w1_in, 16)
            w3 = w_f[:, :].rearrange("p (e h) -> p e h", e=E)
            ve.wait_ge(bias_done, 1)
            after(ve.tensor_tensor(b1T[:, :], bank[7][:, 0:E * HC], cols[:, 0:E * HC], ALU.add))
            for e in range(E):
                ins = ve.tensor_scalar(w3[:, e, :], w3[:, e, :], cols[:, 32 + e:33 + e], None, ALU.mult)
            after(ins)
            after(ve.tensor_reduce(wmax[:, 0:1], w_f[:, :], AX_X, ALU.max, apply_absolute_value=True))
            after(ve.tensor_reduce(wmax[:, 1:2], b1T[:, :], AX_X, ALU.max, apply_absolute_value=True))

            def split(dst, src, scale):
                n = E * H // 4
                for i in range(4):
                    a, b = i * n, (i + 1) * n
                    ins = ve.tensor_scalar(dst[:, 0, a:b], src[:, a:b], scale, None, ALU.mult)
                after(ins)
                for i in range(4):
                    a, b = i * n, (i + 1) * n
                    ins = ve.scalar_tensor_tensor(dst[:, 1, a:b], src[:, a:b], scale, dst[:, 0, a:b], ALU.mult, ALU.subtract)
                return ins

            tell(ve.memset(wmax[:, 2:4], 0.0), wmax_ready)
            ve.wait_ge(wtop_ready, 1)
            after(ve.scalar_tensor_tensor(wtop[:, 1:2], wtop[:, 0:1], float(D), wtop[:, 1:2], ALU.mult, ALU.add))
            after(ve.tensor_scalar(wtop[:, 0:2], wtop[:, 0:2], 1e-30, None, ALU.max))
            after(ve.tensor_scalar(pow2[:, 0:2].bitcast(U32), wtop[:, 0:2].bitcast(U32), 0x7F800000, None, ALU.bitwise_and))
            after(ve.reciprocal(scl[:, 0:2], pow2[:, 0:2]))
            after(ve.tensor_scalar(scl[:, 0:2], scl[:, 0:2], float(2 ** 14), None, ALU.mult))
            after(ve.tensor_scalar(scl[:, 2:3], pow2[:, 0:1], 2.0 ** -(14 + SX), None, ALU.mult))
            tell(split(w1p, w_f, scl[:, 0:1]), w2_free)
            ve.wait_ge(w2_in, 16 * E)
            tell(ve.tensor_reduce(wmax[:, 2:3], w_f[:, :], AX_X, ALU.max, apply_absolute_value=True), wmax_ready)
            ve.wait_ge(wtop_ready, 2)
            after(ve.tensor_scalar(wtop[:, 2:3], wtop[:, 2:3], 1e-30, None, ALU.max))
            after(ve.tensor_scalar(pow2[:, 2:3].bitcast(U32), wtop[:, 2:3].bitcast(U32), 0x7F800000, None, ALU.bitwise_and))
            after(ve.reciprocal(scl[:, 3:4], pow2[:, 2:3]))
            after(ve.tensor_scalar(scl[:, 3:4], scl[:, 3:4], float(2 ** 14), None, ALU.mult))
            after(ve.scalar_tensor_tensor(scl[:, 4:5], pow2[:, 1:2], 2.0 ** -28, pow2[:, 2:3], ALU.mult, ALU.mult))
            tell(split(w2p, w_f, scl[:, 3:4]), weights_ready)

            def turn(j, k, it):
                ve.wait_ge(blk_T, j + 1)
                if it is not None or k >= 2:
                    ve.wait_ge(up_done, 2 * j - 2)
                ve.tensor_copy(bT[:, k % 2, :], bank[6 + k % 2][:, 0:P].bitcast(F16)).then_inc(bT_ready, 1)

            def halves(j, k, s, it):
                u, n = 2 * j + s, (2 * k + s) % 4
                ve.wait_ge(gelu_done, u + 1)
                if it is not None or k >= 2:
                    ve.wait_ge(down_done, u - 3)
                ve.tensor_scalar(hp[:, n, 0, :], hf[:, n, :], scl[:, 1:2], None, ALU.mult).then_inc(h_hi, 1)
                ve.wait_ge(h_hi, u + 1)
                ve.scalar_tensor_tensor(hp[:, n, 1, :], hf[:, n, :], scl[:, 1:2], hp[:, n, 0, :],
                                        ALU.mult, ALU.subtract).then_inc(split_done, 1)

            def mix(j, k, s, it):
                u = 2 * j + s
                ve.wait_ge(down_done, u + 1)
                if s == 0:
                    ve.tensor_scalar(wg[:, 2 * k:2 * k + 2], blk[:, k, W_GATE:W_GATE + 2], scl[:, 4:5], None,
                                     ALU.mult).then_inc(wg_ready, 1)
                    ve.wait_ge(wg_ready, j + 1)
                else:
                    ve.wait_ge(mixed, u)
                ve.scalar_tensor_tensor(ob[:, k, :], bank[4 + s][:, 0:D], wg[:, 2 * k + s:2 * k + s + 1],
                                        blk[:, k, W_RES:W_RES + D] if s == 0 else ob[:, k, :],
                                        ALU.mult, ALU.add).then_inc(mixed, 1)

            turn(0, 0, None)

            def blocks(j, k, it):
                if not (isinstance(it, int) and k == UNROLL - 1):
                    turn(j + 1, (k + 1) % UNROLL, it if k + 1 < UNROLL else 0)
                for s in range(2):
                    halves(j, k, s, it)
                    if k > 0:
                        mix(j - 1, k - 1, s, it)
                    elif it is not None:
                        mix(j - 1, UNROLL - 1, s, it - 1)

            unit_loop(ve, blocks)
            for s in range(2):
                mix(NB - 1, UNROLL - 1, s, NIT - 1)

        @block.tensor
        def _(pe):
            pe.wait_ge(consts, 11)
            pe.wait_ge(small_in, 16 * 6)
            pe.wait_ge(dve_stage, 1)
            pe.transpose(bank[7][:, 0:P], stage[:, :], ident[:, :]).then_inc(stage_T, 1)
            pe.wait_ge(gA_ready, 1)
            for k in range(K):
                mm = pe.transpose(bank[k // 4][:, (k % 4) * P:(k % 4 + 1) * P], gA[:, k * P:(k + 1) * P], ident[:, :])
                if k % 4 == 3 or k == K - 1:
                    mm.then_inc(gT_done, 1)
            pe.wait_ge(gNT_ready, 3)
            for h in range(HALF):
                rhs = gNT[:, h * NG * P:(h + 1) * NG * P]
                pe.matmul(bank[3 + h][:, :], gx[:, h, :], rhs[:, 0:4 * P], start=True, stop=True)
                pe.matmul(bank[5 + h][:, 0:P], gx[:, h, :], rhs[:, 4 * P:5 * P], start=True, stop=True).then_inc(xa_done, 1)
            pe.wait_ge(xaT_ready, HALF)
            pe.wait_ge(gw_in, 16 * (5 + NG))
            for n in range(NG * GC):
                g = n // GC
                mm = pe.matmul(bank[n // 2][:, (n % 2) * 256:(n % 2) * 256 + HALF * P], gW1s[:, n * P:(n + 1) * P],
                               xaT[:, g * HALF * P:(g + 1) * HALF * P], start=True, stop=True)
                if n % 2:
                    mm.then_inc(h1_done, 1)
            pe.wait_ge(h1_act, NG * GC)
            pe.wait_ge(cols_ready, 1)
            for k in range(K):
                h, g = k // NG, k % NG
                for c in range(GC):
                    n = (g * GC + c) * HALF + h
                    mm = pe.matmul(bank[5 + k // 4][:, (k % 4) * P:(k % 4 + 1) * P], h1T[:, n * P:(n + 1) * P],
                                   gW2s[:, (g * GC + c) * D:(g * GC + c + 1) * D], start=(c == 0), stop=(c == GC - 1))
                if k % 4 == 3 or k == K - 1:
                    mm.then_inc(s2_done, 1)
            pe.wait_ge(s2_ready, 3)
            for k in range(K):
                o = bank[k // 4][:, (k % 4) * P:(k % 4 + 1) * P]
                pe.matmul(o, gNT[:, k * P:(k + 1) * P], gS2[:, k * P:(k + 1) * P], start=True, stop=False)
                mm = pe.matmul(o, ones[0:1, :], gb2r[0:1, (k % NG) * D:(k % NG + 1) * D], start=False, stop=True)
                if k % 4 == 3 or k == K - 1:
                    mm.then_inc(go_done, 1)

            def turn_tokens(q):
                pe.wait_ge(xt_ready, q + 1)
                if q >= 2:
                    pe.wait_ge(xtT_ready, q - 1)
                for i in range(4):
                    mm = pe.transpose(bank[q % 2][:, i * P:(i + 1) * P], xt[:, 4 * q + i, :], ident[:, :])
                mm.then_inc(xtT_done, 1)

            turn_tokens(0)
            for q in range(T // 4):
                if q + 1 < T // 4:
                    turn_tokens(q + 1)
                pe.wait_ge(xtT_ready, q + 1)
                for i in range(4):
                    t = 4 * q + i
                    pe.matmul(bank[4][:, t * E:(t + 1) * E], rt_buf(q)[:, i * P:(i + 1) * P], wr_sb[:, :],
                              start=True, stop=True).then_inc(logit_done, 1)

            pe.wait_ge(counts_ready, 1)
            pe.matmul(bank[5][:, 0:NCLS], ones16[:, :], before[:, T, :], start=True, stop=True).then_inc(total_done, 1)
            pe.wait_ge(base_ready, 1)
            pe.wait_ge(consts, 13)
            for q in range(8):
                a, b = 8 * q, 8 * q + 8
                pe.matmul(bank[q][:, :], tri[:, :], onehot[:, a:b, :], start=True, stop=False)
                pe.matmul(bank[q][:, :], ones16[:, :], before[:, a:b, :], start=False, stop=False)
                pe.matmul(bank[q][:, :], ones16[:, :],
                          base16[:, :].rearrange("p (o c) -> p o c", o=1).to_broadcast([P, 8, NCLS]),
                          start=False, stop=True).then_inc(rank_done, 1)
            pe.wait_ge(b2x_ready, 1)
            pe.wait_ge(gates_ready, 1)
            for r in range(T // 16):
                pe.transpose(bank[0][:, 0:P], oh1[:, 16 * r:16 * r + 16, :].rearrange("p t e -> p (t e)"),
                             ident[:, :]).then_inc(GT_done, 1)
                pe.wait_ge(GT_ready, r + 1)
                for q in range(4):
                    if r >= 1:
                        pe.wait_ge(bias_added, 4 * (r - 1) + q + 1)
                    pe.matmul(bank[1 + q][:, :], GT[:, :], b2x[:, 4 * q:4 * q + 4, :], start=True, stop=True
                              ).then_inc(bias_sum, 1)
            pe.wait_ge(bcls_ready, 1)
            pe.transpose(bank[6][0:1, 0:P], bcls[:, 0:1], ident[:, :]).then_inc(bcls_T, 1)
            pe.wait_ge(w1_in, 16)
            for e in range(E):
                for c in range(HC):
                    n = e * HC + c
                    mm = pe.matmul(bank[7][:, n:n + 1], w_f[:, n * P:(n + 1) * P], cols[:, 40 + e:41 + e],
                                   start=True, stop=True)
            mm.then_inc(bias_done, 1)

            pe.wait_ge(table_ready, 1)
            pe.wait_ge(weights_ready, 1)

            def turn_rows(j, k, it):
                pe.wait_ge(blk_in[k], 16 if it is None else 16 * (it + 1))
                if it is not None or k >= 2:
                    pe.wait_ge(bT_ready, j - 1)
                for a in range(2):
                    mm = pe.transpose(bank[6 + k % 2][:, a * D // 2:(a + 1) * D // 2].bitcast(F16),
                                      blk[:, k, a * D // 2:(a + 1) * D // 2].bitcast(F16), ident16[:, :])
                mm.then_inc(blk_T, 1)

            def up(j, k, s, it):
                u, n = 2 * j + s, (2 * k + s) % 4
                e = pe.value_load(blk_e[0:1, bass.ds(u, 1)], min_val=0, max_val=E - 1)
                e = pe.snap(e * H)
                pe.wait_ge(bT_ready, j + 1)
                if it is not None or k >= 2:
                    pe.wait_ge(gelu_done, u - 3)
                pe.wait_ge(table_ready, 1)
                for c in range(HC):
                    for m, (wa, xa) in enumerate(((0, 0), (0, 1), (1, 0))):
                        mm = pe.matmul(bank[n][:, c * P:(c + 1) * P], w1p[:, wa, bass.ds(e + c * P, P)],
                                       bT[:, k % 2, xa * D:(xa + 1) * D], start=(m == 0), stop=(m == 2))
                mm.then_inc(up_done, 1)

            def down(j, k, s, it):
                u, n = 2 * j + s, (2 * k + s) % 4
                e = pe.value_load(blk_e[0:1, bass.ds(u, 1)], min_val=0, max_val=E - 1)
                e = pe.snap(e * H)
                pe.wait_ge(split_done, u + 1)
                if it is not None or k >= 1:
                    pe.wait_ge(mixed, u - 1)
                pe.wait_ge(table_ready, 1)
                for c in range(HC):
                    for m, (wa, ha) in enumerate(((0, 0), (1, 0), (0, 1))):
                        mm = pe.matmul(bank[4 + s][:, 0:D], hp[:, n, ha, c * P:(c + 1) * P],
                                       w2p[:, wa, bass.ds(e + c * P, P)], start=(c == 0 and m == 0),
                                       stop=(c == HC - 1 and m == 2))
                mm.then_inc(down_done, 1)

            turn_rows(0, 0, None)

            def blocks(j, k, it):
                if k + 1 < UNROLL:
                    turn_rows(j + 1, k + 1, it)
                elif not isinstance(it, int):
                    turn_rows(j + 1, 0, 1 if it is None else it + 1)
                for s in range(2):
                    up(j, k, s, it)
                    if k > 0:
                        down(j - 1, k - 1, s, it)
                    elif it is not None:
                        down(j - 1, UNROLL - 1, s, 0)

            unit_loop(pe, blocks)
            for s in range(2):
                down(NB - 1, UNROLL - 1, s, 0)


_INS = ['x', 'adj', 'L0_gnn_W1', 'L0_gnn_b1', 'L0_gnn_W2', 'L0_gnn_b2', 'L0_gnn_fusion_w', 'L0_ffn_Wr',
        'L0_ffn_br', 'L0_ffn_ln_g', 'L0_ffn_ln_b', 'L0_ffn_W1', 'L0_ffn_b1', 'L0_ffn_W2', 'L0_ffn_b2']


def kernel(**inputs):
    import numpy as _np
    import concourse.bacc as _bacc
    from concourse import mybir as _mybir
    from concourse.bass_utils import run_bass_kernel_spmd as _run

    nc = _bacc.Bacc("TRN2", target_bir_lowering=False, num_devices=1)
    arrays = {f"in_{name}_dram": _np.ascontiguousarray(inputs[name]) for name in _INS}
    arrays["group_pairs_dram"], arrays["group_members_dram"] = group_tables()
    args = [nc.dram_tensor(name, a.shape, _mybir.dt.from_np(a.dtype), kind="ExternalInput").ap()
            for name, a in arrays.items()]
    out = nc.dram_tensor("out_0_dram", inputs["x"].shape, _mybir.dt.float32, kind="ExternalOutput").ap()
    build(nc, *args, out)
    r = _run(nc, [arrays], core_ids=[0])
    return r.results[0]["out_0_dram"]
```

```python
from contextlib import ExitStack

import numpy as np

import concourse.bass as bass
import concourse.mybir as mybir

ALU = mybir.AluOpType
ACT = mybir.ActivationFunctionType
F32 = mybir.dt.float32
F16 = mybir.dt.float16
BF16 = mybir.dt.bfloat16
I32 = mybir.dt.int32
U32 = mybir.dt.uint32
AX_X = mybir.AxisListType.X

P = 128
GROUPS = [list(range(25)), [0, 1, 2, 3, 4, 5, 6, 7, 8], [0, 9, 10, 11, 12, 13, 14],
          [6, 7, 8, 12, 13, 14], [3, 4, 5, 9, 10, 11]]
NODES = 25
SLOT = 32
EPS = 1e-5

W_ID = 128
W_ROW = 129
NO_TOKEN = 1 << 20
HALVES = 2
UNIT = HALVES * P
UNROLL = 6
SX = 11


def group_tables():
    member = np.zeros((P, len(GROUPS)), np.float32)
    for g, nodes in enumerate(GROUPS):
        for j in range(P // SLOT):
            member[[SLOT * j + n for n in nodes], g] = 1.0
    both = member[:, :, None] * member.T[None, :, :]
    return np.ascontiguousarray(both.reshape(P, -1)), member


def units_bound(tokens, experts):
    bound = (2 * tokens + experts * (UNIT - 1)) // UNIT
    return -(-bound // UNROLL) * UNROLL


def build(nc, x, adj, gW1, gb1, gW2, gb2, fusion, Wr, br, ln_g, ln_b, W1, b1, W2, b2,
          both_in, member_in, out):
    B, S, D = x.shape
    E, _, H = W1.shape
    NG, _, GH = gW1.shape
    assert D == P
    N = B * S
    T = N // P
    HC = H // P
    GC = GH // P
    NU = units_bound(N, E)
    NIT = NU // UNROLL
    CAP = N + UNIT
    HALF = B * SLOT // P
    BPH = P // SLOT
    K = NG * HALF
    NS = S // P
    LAST = NS - 1

    def tile_of(g):
        return (g + 1) % NS

    x_tiles = x.rearrange("b (j p) d -> j p b d", p=P)
    out_tiles = out.rearrange("b (j p) d -> j p b d", p=P)
    pool = nc.dram_tensor("pool", [E * CAP + UNIT, W_ROW], F32, kind="Internal").ap()
    picked = nc.dram_tensor("picked", [2 * N, D], F32, kind="Internal").ap()
    picked_tiles = picked.rearrange("(b j p two) d -> j p b (two d)", b=B, p=P, two=2)

    with ExitStack() as ctx:
        def sb(name, shape, dt=F32):
            return ctx.enter_context(nc.sbuf_tensor(name, shape, dt))

        def sem(name):
            return ctx.enter_context(nc.semaphore(name))

        bank = [ctx.enter_context(nc.psum_tensor(f"bank{i}", [P, 512], F32)) for i in range(8)]

        res = sb("res", [P, NS, B, D])
        rows = sb("rows", [P, NS, B, W_ROW])
        parts = rows[:, :, :, 0:D].bitcast(F16)
        hi_part, lo_part = parts[:, :, :, 0:D], parts[:, :, :, D:2 * D]
        ids = rows[:, :, :, W_ID:W_ID + 1].bitcast(I32)
        xt = sb("xt", [P, 2, B, D])
        xn = sb("xn", [P, B, D])
        xtT = sb("xtT", [P, B * P])
        stats = sb("stats", [P, 2, B, 6])
        norm = sb("norm", [P, 4, 5, B])
        fill = sb("fill", [P, HALVES * W_ROW])

        ident = sb("ident", [P, P])
        ident16 = sb("ident16", [P, P], F16)
        ones = sb("ones", [P, P])
        ones16 = sb("ones16", [P, P], BF16)
        tri = sb("tri", [P, P], BF16)
        e_less = sb("e_less", [P, E])
        e_start = sb("e_start", [P, E])
        unit_no = sb("unit_no", [1, NU])
        delta = sb("delta", [P, 2 * B])

        stage = sb("stage", [P, P])
        cols = sb("cols", [P, 64])
        w1f = sb("w1f", [P, E * H])
        w2f = sb("w2f", [P, E * H])
        w1p = sb("w1p", [P, E * HC * 2 * P], F16)
        w2p = sb("w2p", [P, E * HC * 2 * P], F16)
        b1T = sb("b1T", [P, E * HC])
        wmax = sb("wmax", [P, 4])
        wtop = sb("wtop", [P, 4])
        wdiag = sb("wdiag", [4, 8])
        pow2 = sb("pow2", [P, 4])
        scl = sb("scl", [P, 8])
        wr_sb = sb("wr_sb", [P, E])
        br_b = sb("br_b", [P, E])
        b2rep = sb("b2rep", [P, D])

        logit = sb("logit", [P, B, E])
        eq = sb("eq", [P, B, E])
        best = sb("best", [P, B])
        top = sb("top", [P, 2, T])
        oh = sb("oh", [P, NS, B, 2, E])
        onehot = sb("onehot", [P, NS, B, E], BF16)
        count = sb("count", [P, E])
        counted = sb("counted", [P, NS + 1, E], BF16)
        place = sb("place", [P, B, E])
        chosen = sb("chosen", [P, B, 2, E])
        posf = sb("posf", [P, B, 2])
        pos = sb("pos", [P, NS, B, 2], U32)
        gate = sb("gate", [P, 3, T])
        goh = sb("goh", [P, NS, B, E])
        ct = sb("ct", [1, 6, E])
        ct_i = sb("ct_i", [1, 2, E], I32)
        cmp = sb("cmp", [1, NU, E])
        ut = sb("ut", [1, 4, NU])
        unit_row = sb("unit_row", [1, NU], I32)
        unit_w = sb("unit_w", [1, NU], I32)
        unit_b = sb("unit_b", [1, NU], I32)
        gx = sb("gx", [P, HALF, D])
        gsmall = sb("gsmall", [P, 64])
        gmean, gvar, grstd, gtmp = (gsmall[:, 2 * i:2 * i + 2] for i in range(4))
        gdeg, gdinv, gzero, gsafe = (gsmall[:, 10 + 10 * i:20 + 10 * i] for i in range(4))
        gstats = sb("gstats", [P, HALF, 6])
        fus = sb("fus", [P, NG])
        member = sb("member", [P, NG])
        gsc = sb("gsc", [P, 4])
        gb2r = sb("gb2r", [1, NG * D])
        gadd = sb("gadd", [NODES, B, D])

        SHARED = 8716
        shared = sb("shared", [P, SHARED])

        def carver(limit):
            at = [0]

            def take(n):
                at[0] += n
                assert at[0] <= limit
                return shared[:, at[0] - n:at[0]]
            return take

        take = carver(SHARED)
        gW1s = take(NG * GH)
        gW2s = take(NG * GC * D)
        gNT = take(K * P)
        gA = take(K * P)
        xaT = take(K * P)
        h1T = w2p[:, :].bitcast(F32)[:, 0:NG * GC * HALF * P]
        gboth = take(NG * P)
        gZ = take(HALF * P)
        gS2 = gA
        gF = xaT
        gout = take(HALF * D).rearrange("p (h d) -> p h d", h=HALF)

        take = carver(SHARED)
        NB = UNROLL
        blk = take(NB * HALVES * W_ROW).rearrange("p (k w) -> p k w", k=NB)
        bT = take(2 * UNIT).bitcast(F16).rearrange("p (k w) -> p k w", k=2)
        hf = take(2 * HC * UNIT).rearrange("p (k h) -> p k h", k=2)
        hp = take(3 * HC * UNIT).bitcast(F16).rearrange("p (k a h) -> p k a h", k=3, a=2)
        ob = take(NB * UNIT).rearrange("p (k a d) -> p k a d", k=NB, a=HALVES)

        YB = 3
        take = carver(SHARED)
        yb = take(YB * B * 2 * D).rearrange("p (k b w) -> p k b w", k=YB, b=B)
        b2x = take(2 * B * D).rearrange("p (t d) -> p t d", t=2 * B)
        GT = sb("GT", [P, P])

        x_in = [sem(f"x_in{i}") for i in range(NS)]
        gx_in = sem("gx_in")
        gadj_in = sem("gadj_in")
        gw_in = sem("gw_in")
        small_in = sem("small_in")
        w1_in = sem("w1_in")
        w2_in = sem("w2_in")
        b2_in = sem("b2_in")
        gadd_in = sem("gadd_in")
        zeroed = sem("zeroed")
        ranks_consts = sem("ranks_consts")
        consts = sem("consts")
        filled = sem("filled")
        v = sem("v")
        dve_stage = sem("dve_stage")
        fus_max = sem("fus_max")
        fus_exp = sem("fus_exp")
        gsqrt_in = sem("gsqrt_in")
        gsqrt_out = sem("gsqrt_out")
        gA_ready = sem("gA_ready")
        gT_done = sem("gT_done")
        gNT_ready = sem("gNT_ready")
        xa_done = sem("xa_done")
        xaT_ready = sem("xaT_ready")
        h1_done = sem("h1_done")
        h1_act = sem("h1_act")
        s2_done = sem("s2_done")
        s2_ready = sem("s2_ready")
        go_done = sem("go_done")
        gout_ready = sem("gout_ready")
        stage_T = sem("stage_T")
        cols_ready = sem("cols_ready")
        sqrt1_in = sem("sqrt1_in")
        sqrt1_out = sem("sqrt1_out")
        sqrt2_in = sem("sqrt2_in")
        sqrt2_out = sem("sqrt2_out")
        xt_ready = sem("xt_ready")
        xtT_done = sem("xtT_done")
        xtT_ready = sem("xtT_ready")
        logit_done = sem("logit_done")
        logit_read = sem("logit_read")
        norm2_ready = sem("norm2_ready")
        xn_ready = sem("xn_ready")
        split_x = sem("split_x")
        onehot_ready = sem("onehot_ready")
        rank_done = sem("rank_done")
        pos_ready = sem("pos_ready")
        ids_ready = sem("ids_ready")
        sent_first = [sem(f"sent_first{i}") for i in range(2)]
        sent_second = sem("sent_second")
        padded = sem("padded")
        total_done = sem("total_done")
        table_ready = sem("table_ready")
        gates_in = sem("gates_in")
        gates_exp = sem("gates_exp")
        bias_done = sem("bias_done")
        folded = sem("folded")
        wmax_ready = sem("wmax_ready")
        wmax_T = sem("wmax_T")
        wdiag_ready = sem("wdiag_ready")
        wtop_done = sem("wtop_done")
        scales_ready = sem("scales_ready")
        whi_ready = sem("whi_ready")
        weights_ready = sem("weights_ready")
        blk_in = [sem(f"blk_in{k}") for k in range(NB)]
        blk_T = sem("blk_T")
        bT_ready = sem("bT_ready")
        up_done = sem("up_done")
        gelu_done = sem("gelu_done")
        hi_done = sem("hi_done")
        split_done = sem("split_done")
        down_done = sem("down_done")
        half_out = sem("half_out")
        evacuated = sem("evacuated")
        storing = sem("storing")
        stored = [sem(f"stored{k}") for k in range(NB)]
        b2x_ready = sem("b2x_ready")
        GT_done = sem("GT_done")
        GT_ready = sem("GT_ready")
        bias_sum = sem("bias_sum")
        bias_added = sem("bias_added")
        y_in = [sem(f"y_in{k}") for k in range(YB)]
        summed = sem("summed")
        out_sent = sem("out_sent")

        block = ctx.enter_context(nc.Block())

        def unit_loop(eng, step):
            for k in range(UNROLL):
                step(k, k, None)
            with eng.Fori(1, NIT - 1) as it:
                for k in range(UNROLL):
                    step(it * UNROLL + k, k, it)
            for k in range(UNROLL):
                step((NIT - 1) * UNROLL + k, k, NIT - 1)

        @block.sync
        def _(sp):
            sp.dma_start(res[:, 0], x_tiles[tile_of(0)]).then_inc(x_in[0], 16)
            sp.wait_ge(zeroed, 2)
            for b in range(B):
                p0 = SLOT * (b % BPH)
                sp.dma_start(gx[p0:p0 + NODES, b // BPH, :], x[b, 0:NODES, :]).then_inc(gx_in, 16)
            for b in range(B):
                p0 = SLOT * (b % BPH)
                c0 = (b // BPH) * P + p0
                sp.dma_start(gZ[p0:p0 + NODES, c0:c0 + NODES], adj[b, 0:NODES, 0:NODES]).then_inc(gadj_in, 16)
            for g in range(1, NS):
                sp.dma_start(res[:, g], x_tiles[tile_of(g)]).then_inc(x_in[g], 16)
            sp.dma_start(w1f[:, :].rearrange("p (e h) -> p e h", e=E), W1.rearrange("e d h -> d e h")).then_inc(w1_in, 16)
            for e in range(E):
                sp.dma_start(w2f[:, e * H:(e + 1) * H].rearrange("p (c d) -> p c d", c=HC),
                             W2[e].rearrange("(c p) d -> p c d", p=P)).then_inc(w2_in, 16)
            for i in range(P // E):
                sp.dma_start(b2rep[i * E:(i + 1) * E, :], b2).then_inc(b2_in, 16)
            sp.wait_ge(filled, 2)
            sp.dma_start(pool[E * CAP:E * CAP + UNIT, :].rearrange("(p a) w -> p (a w)", p=P), fill[:, :]
                         ).then_inc(padded, 16)
            sp.wait_ge(gout_ready, 1)
            for b in range(B):
                p0 = SLOT * (b % BPH)
                sp.dma_start(gadd[:, b, :], gout[p0:p0 + NODES, b // BPH, :]).then_inc(gadd_in, 16)
            sp.wait_ge(table_ready, 1)
            for e in range(E):
                row = sp.value_load(ct_i[0:1, 1, e:e + 1], min_val=0, max_val=E * CAP)
                sp.dma_start(pool[bass.ds(row, UNIT), :].rearrange("(p a) w -> p (a w)", p=P), fill[:, :]
                             ).then_inc(padded, 16)
            for i in range(2):
                sp.wait_ge(sent_first[i], 16 * T // 2)
            sp.wait_ge(sent_second, 16 * T)
            sp.wait_ge(padded, 16 * (E + 1))

            def load(u, k, it):
                row = sp.value_load(unit_row[0:1, bass.ds(u, 1)], min_val=0, max_val=E * CAP)
                if it is not None:
                    sp.wait_ge(stored[k], 16 * HALVES * it)
                sp.dma_start(blk[:, k, :], pool[bass.ds(row, UNIT), :].rearrange("(p a) w -> p (a w)", p=P)
                             ).then_inc(blk_in[k], 16)

            unit_loop(sp, load)

            for k in range(NB):
                sp.wait_ge(stored[k], 16 * HALVES * NIT)
            sp.wait_ge(evacuated, NU)
            for g in range(NS):
                if g >= YB:
                    sp.wait_ge(summed, g - YB + 1)
                for h in range(2):
                    b0, b1_ = h * B // 2, (h + 1) * B // 2
                    sp.dma_start(yb[:, g % YB, b0:b1_, :], picked_tiles[tile_of(g)][:, b0:b1_, :]).then_inc(y_in[g % YB], 16)

        @block.gpsimd
        def _(po):
            po.memset(ones16[:, :], 1.0).then_inc(ranks_consts, 1)
            po.memset(tri[:, :], 1.0).then_inc(ranks_consts, 1)
            po.memset(ident[:, :], 0.0).then_inc(consts, 1)
            po.memset(ident16[:, :], 0.0).then_inc(consts, 1)
            po.memset(delta[:, :], 1.0).then_inc(consts, 1)
            po.iota(e_less[:, :], [[1, E]], base=-E, channel_multiplier=0,
                    allow_small_or_imprecise_dtypes=True).then_inc(ranks_consts, 1)
            po.iota(e_start[:, :], [[CAP, E]], base=0, channel_multiplier=0,
                    allow_small_or_imprecise_dtypes=True).then_inc(ranks_consts, 1)
            po.wait_ge(ranks_consts, 4)
            po.affine_select(out=tri[:, :], in_=tri[:, :], compare_op=ALU.is_gt, fill=0.0, base=0,
                             pattern=[[1, P]], channel_multiplier=-1).then_inc(ranks_consts, 1)
            po.wait_ge(consts, 3)
            for m in (ident, ident16):
                po.affine_select(out=m[:, :], in_=m[:, :], compare_op=ALU.not_equal, fill=1.0, base=0,
                                 pattern=[[-1, P]], channel_multiplier=1).then_inc(consts, 1)
            po.affine_select(out=delta[:, :], in_=delta[:, :], compare_op=ALU.is_ge, fill=0.0, base=0,
                             pattern=[[-E, 2 * B]], channel_multiplier=1).then_inc(consts, 1)
            po.wait_ge(consts, 6)
            po.affine_select(out=delta[:, :], in_=delta[:, :], compare_op=ALU.is_ge, fill=0.0, base=E - 1,
                             pattern=[[E, 2 * B]], channel_multiplier=-1).then_inc(consts, 1)
            po.memset(fill[:, :], 0.0).then_inc(filled, 1)
            po.wait_ge(filled, 1)
            po.iota(fill[:, :].rearrange("p (a w) -> p a w", a=HALVES)[:, :, W_ID:W_ID + 1].bitcast(I32), [[0, HALVES]],
                    base=NO_TOKEN, channel_multiplier=0).then_inc(filled, 1)
            po.iota(unit_no[:, :], [[1, NU]], base=0, channel_multiplier=0,
                    allow_small_or_imprecise_dtypes=True).then_inc(filled, 1)

            def number(g, which):
                po.iota(ids[:, g], [[2 * S, B]], base=2 * P * tile_of(g) + which, channel_multiplier=2
                        ).then_inc(ids_ready, 1)
                po.wait_ge(ids_ready, made[0] + 1)
                made[0] += 1

            made = [0]

            def send(g, which):
                for b in range(B):
                    po.indirect_dma_start(pool, bass.IndirectOffsetOnAxis(ap=pos[:, g, b, which:which + 1], axis=0),
                                          rows[:, g, b, :], None, bounds_check=E * CAP - 1,
                                          oob_is_err=False).then_inc(sent_second if which else sent_first[g % 2], 16)

            for g in range(NS):
                number(g, 0)
            for g in range(NS + 1):
                if g < NS:
                    po.wait_ge(pos_ready, g + 1)
                    po.wait_ge(split_x, g + 1)
                    send(g, 0)
                if g > 0:
                    po.wait_ge(sent_first[(g - 1) % 2], 16 * B * ((g - 1) // 2 + 1))
                    number(g - 1, 1)
                    send(g - 1, 1)

            def store(u, k, it):
                po.wait_ge(evacuated, u + 1)
                po.sem_inc(storing, 1)
                for a in range(HALVES):
                    w = a * W_ROW + W_ID
                    po.indirect_dma_start(picked, bass.IndirectOffsetOnAxis(
                        ap=blk[:, k, w:w + 1].bitcast(U32), axis=0), ob[:, k, a, :], None,
                        bounds_check=2 * N - 1, oob_is_err=False).then_inc(stored[k], 16)

            unit_loop(po, store)

        @block.scalar
        def _(act):
            act.wait_ge(dve_stage, 1)
            act.dma_start(stage[0:E * HC, :], b1.rearrange("e (c h) -> (e c) h", h=P)).then_inc(small_in, 16)
            act.dma_start(stage[32:32 + E, :], ln_g).then_inc(small_in, 16)
            act.dma_start(stage[40:40 + E, :], ln_b).then_inc(small_in, 16)
            act.dma_start(stage[48:48 + NG * GC, :], gb1.rearrange("g (c h) -> (g c) h", h=P)).then_inc(small_in, 16)
            act.dma_start(wr_sb[:, :], Wr).then_inc(small_in, 16)
            act.dma_start(br_b[:, :], br.rearrange("(o e) -> o e", o=1).to_broadcast([P, E])).then_inc(small_in, 16)
            act.dma_start(fus[:, :], fusion.rearrange("(o g) -> o g", o=1).to_broadcast([P, NG])).then_inc(gw_in, 16)
            act.dma_start(member[:, :], member_in).then_inc(gw_in, 16)
            act.dma_start(gboth, both_in).then_inc(gw_in, 16)
            act.dma_start(gW1s.rearrange("p (g h) -> p g h", g=NG), gW1.rearrange("g d h -> d g h")).then_inc(gw_in, 16)
            for g in range(NG):
                act.dma_start(gW2s[:, g * GC * D:(g + 1) * GC * D].rearrange("p (c d) -> p c d", c=GC),
                              gW2[g].rearrange("(c p) d -> p c d", p=P)).then_inc(gw_in, 16)
            act.dma_start(gb2r[:, :], gb2.rearrange("(o g) d -> o (g d)", o=1)).then_inc(gw_in, 16)
            act.wait_ge(fus_max, 1)
            act.activation(fus[:, :], fus[:, :], ACT.Exp, bias=gsc[:, 0:1], accum_out=gsc[:, 1:2]).then_inc(fus_exp, 1)

            def gnn_root(n):
                act.wait_ge(gsqrt_in, n + 1)
                if n == 0:
                    act.activation(grstd, gtmp, ACT.Sqrt).then_inc(gsqrt_out, 1)
                else:
                    act.activation(gdinv, gsafe, ACT.Sqrt).then_inc(gsqrt_out, 1)

            def gnn_hidden():
                act.wait_ge(cols_ready, 1)
                for n in range(NG * GC):
                    if n % 2 == 0:
                        act.wait_ge(h1_done, n // 2 + 1)
                    act.activation(h1T[:, n * HALF * P:(n + 1) * HALF * P],
                                   bank[n // 2][:, (n % 2) * 256:(n % 2) * 256 + HALF * P],
                                   ACT.Relu, bias=cols[:, 48 + n:49 + n]).then_inc(h1_act, 1)

            def root1(g):
                act.wait_ge(sqrt1_in, g + 1)
                act.activation(norm[:, g % 2, 2, :], norm[:, g % 2, 3, :], ACT.Sqrt).then_inc(sqrt1_out, 1)

            def root2(g):
                act.wait_ge(sqrt2_in, g + 1)
                act.activation(norm[:, 2 + g % 2, 2, :], norm[:, 2 + g % 2, 3, :], ACT.Sqrt).then_inc(sqrt2_out, 1)

            def copy_tokens(g):
                for h in range(2):
                    act.wait_ge(xtT_done, 2 * g + h + 1)
                    if g >= 1 and h == 0:
                        act.wait_ge(logit_done, g)
                    act.activation(xtT[:, h * 512:(h + 1) * 512], bank[5][:, :], ACT.Copy).then_inc(xtT_ready, 1)

            def normalise(g):
                act.wait_ge(norm2_ready, g + 1)
                for b in range(B):
                    ins = act.activation(xn[:, b, :], xt[:, g % 2, b, :], ACT.Identity,
                                         bias=norm[:, 2 + g % 2, 4, b:b + 1], scale=norm[:, 2 + g % 2, 2, b:b + 1])
                ins.then_inc(xn_ready, 1)

            def fold():
                act.wait_ge(bias_done, 1)
                for e in range(E):
                    ins = act.activation(w1f[:, e * H:(e + 1) * H], w1f[:, e * H:(e + 1) * H], ACT.Copy,
                                         scale=cols[:, 32 + e:33 + e])
                ins.then_inc(folded, 1)

            def weight_parts():
                act.wait_ge(scales_ready, 1)
                for dst, src, s in ((w1p, w1f, 0), (w2p, w2f, 3)):
                    to = dst[:, :].rearrange("p (n a d) -> p n a d", a=2, d=P)[:, :, 0, :]
                    act.activation(to, src[:, :].rearrange("p (n d) -> p n d", d=P), ACT.Copy,
                                   scale=scl[:, s:s + 1]).then_inc(whi_ready, 1)

            for n in range(NS + 3):
                if n == 1:
                    gnn_root(0)
                if n == 1:
                    gnn_root(1)
                if 2 <= n < NS + 2:
                    normalise(n - 2)
                if n == 3:
                    gnn_hidden()
                if n == 5:
                    fold()
                if 1 <= n < NS + 1:
                    root2(n - 1)
                if n < NS:
                    root1(n)
                if 1 <= n < NS + 1:
                    copy_tokens(n - 1)
            weight_parts()
            act.wait_ge(gates_in, 1)
            act.activation(gate[:, 2, :], gate[:, 2, :], ACT.Exp).then_inc(gates_exp, 1)
            act.wait_ge(table_ready, 1)

            def gelus(u, k, it):
                first = act.value_load(unit_b[0:1, bass.ds(u, 1)], min_val=0, max_val=(E - 1) * HC)
                act.wait_ge(up_done, u + 1)
                if it is not None or k >= 2:
                    act.wait_ge(split_done, u - 1)
                for c in range(HC):
                    ins = act.activation(hf[:, k % 2, c * UNIT:(c + 1) * UNIT],
                                         bank[2 * (k % 2) + c // 2][:, (c % 2) * UNIT:(c % 2 + 1) * UNIT], ACT.Gelu,
                                         bias=b1T[:, bass.ds(first + c, 1)], scale=scl[:, 2:3])
                ins.then_inc(gelu_done, 1)
                act.wait_ge(gelu_done, u + 1)
                if it is not None or k >= 3:
                    act.wait_ge(down_done, u - 2)
                act.wait_ge(table_ready, 1)
                act.activation(hp[:, k % 3, 0, :], hf[:, k % 2, :], ACT.Copy, scale=scl[:, 1:2]).then_inc(hi_done, 1)

            unit_loop(act, gelus)

            for g in range(NS):
                act.wait_ge(summed, g + 1)
                act.dma_start(out_tiles[tile_of(g)], res[:, g]).then_inc(out_sent, 16)
            act.wait_ge(out_sent, 16 * NS)

        @block.vector
        def _(ve):
            made = [0]

            def after(ins):
                made[0] += 1
                ins.then_inc(v, 1)
                ve.wait_ge(v, made[0])

            told = {}

            def tell(ins, s):
                told[s.name] = told.get(s.name, 0) + 1
                ins.then_inc(s, 1)
                ve.wait_ge(s, told[s.name])

            def newton(r, y, tmp):
                after(ve.tensor_tensor(tmp, r, r, ALU.mult))
                after(ve.scalar_tensor_tensor(tmp, tmp, -0.5, y, ALU.mult, ALU.mult))
                after(ve.scalar_tensor_tensor(r, tmp, 1.5, r, ALU.add, ALU.mult))

            def moments(st, mean_, var_, tmp_, need_sqrt):
                ve.tensor_tensor(mean_, st[:, :, 1], st[:, :, 4], ALU.add)
                ve.tensor_tensor(tmp_, st[:, :, 1], st[:, :, 4], ALU.subtract)
                after(ve.tensor_tensor(var_, st[:, :, 2], st[:, :, 5], ALU.add))
                ve.tensor_scalar(mean_, mean_, 0.5, None, ALU.mult)
                ve.tensor_scalar(var_, var_, 1.0 / D, EPS, ALU.mult, ALU.add)
                after(ve.scalar_tensor_tensor(tmp_, tmp_, 0.25, tmp_, ALU.mult, ALU.mult))
                after(ve.tensor_tensor(var_, var_, tmp_, ALU.add))
                tell(ve.reciprocal(tmp_, var_), need_sqrt)

            tell(ve.memset(stage[:, :], 0.0), dve_stage)
            ve.memset(gx[:, :, :], 0.0).then_inc(zeroed, 1)
            ve.memset(gZ, 0.0).then_inc(zeroed, 1)
            ve.memset(ones[:, :], 1.0)
            ve.memset(wmax[:, :], 0.0)
            after(ve.memset(counted[:, 0, :], 0.0))

            def spread(a, n):
                return a.rearrange("p (k o) -> p k o", o=1).to_broadcast([P, n, P])

            gA3 = gA.rearrange("p (k m) -> p k m", k=K)

            def gnn_moments():
                ve.wait_ge(gx_in, 16 * B)
                for h in range(HALF):
                    ins = ve.bn_stats(gstats[:, h, :], gx[:, h, :])
                after(ins)
                moments(gstats[:, :, :], gmean, gvar, gtmp, gsqrt_in)

            def gnn_degrees():
                ve.wait_ge(gadj_in, 16 * B)
                ve.wait_ge(consts, 5)
                ve.wait_ge(gw_in, 16 * (5 + NG))
                gA4 = gA.rearrange("p (h g m) -> p h g m", h=HALF, g=NG)
                for h in range(HALF):
                    ins = ve.tensor_tensor(gZ[:, h * P:(h + 1) * P], gZ[:, h * P:(h + 1) * P], ident[:, :], ALU.add)
                after(ins)
                for h in range(HALF):
                    ins = ve.tensor_tensor(gA4[:, h], gZ[:, h * P:(h + 1) * P].rearrange("p (o m) -> p o m", o=1).to_broadcast([P, NG, P]),
                                           gboth.rearrange("p (g m) -> p g m", g=NG), ALU.mult)
                after(ins)
                after(ve.tensor_reduce(gdeg, gA3, AX_X, ALU.add))
                after(ve.tensor_scalar(gzero, gdeg, 0.0, None, ALU.is_equal))
                after(ve.tensor_tensor(gdeg, gdeg, gzero, ALU.add))
                tell(ve.reciprocal(gsafe, gdeg), gsqrt_in)
                ve.wait_ge(gsqrt_out, 1)
                newton(grstd, gvar, gtmp)
                for h in range(HALF):
                    ins = ve.tensor_scalar(gx[:, h, :], gx[:, h, :], gmean[:, h:h + 1], grstd[:, h:h + 1],
                                           ALU.subtract, ALU.mult)
                after(ins)

            def gnn_scale():
                ve.wait_ge(gsqrt_out, 2)
                newton(gdinv, gdeg, gsafe)
                after(ve.tensor_scalar(gzero, gzero, -1.0, 1.0, ALU.mult, ALU.add))
                after(ve.tensor_tensor(gdinv, gdinv, gzero, ALU.mult))
                tell(ve.tensor_tensor(gA3, gA3, spread(gdinv, K), ALU.mult), gA_ready)

            def gnn_transposed():
                gN3 = gNT.rearrange("p (k m) -> p k m", k=K)
                for q in range(3):
                    n = min(4, K - 4 * q)
                    ve.wait_ge(gT_done, q + 1)
                    ve.tensor_tensor(gN3[:, 4 * q:4 * q + n], bank[q][:, 0:n * P].rearrange("p (k m) -> p k m", k=n),
                                     spread(gdinv[:, 4 * q:4 * q + n], n), ALU.mult).then_inc(gNT_ready, 1)

            def gnn_inputs():
                xa4 = xaT.rearrange("p (g h m) -> p g h m", g=NG, h=HALF)
                for h in range(HALF):
                    ve.wait_ge(xa_done, h + 1)
                    ve.tensor_copy(xa4[:, 0:4, h, :], bank[3 + h][:, :].rearrange("p (g m) -> p g m", g=4)).then_inc(xaT_ready, 1)
                    ve.tensor_copy(xa4[:, 4, h, :], bank[2][:, 256 + h * P:256 + (h + 1) * P]).then_inc(xaT_ready, 1)

            def gnn_support():
                for q in range(3):
                    n = min(4, K - 4 * q)
                    ve.wait_ge(s2_done, q + 1)
                    ve.tensor_copy(gS2[:, 4 * q * P:(4 * q + n) * P], bank[q][:, 0:n * P]).then_inc(s2_ready, 1)

            def gnn_out(k):
                return bank[3 + k // 4][:, (k % 4) * P:(k % 4 + 1) * P] if k < 8 else bank[2][:, 256 + (k - 8) * P:256 + (k - 7) * P]

            def gnn_mix():
                ve.wait_ge(fus_exp, 1)
                after(ve.reciprocal(gsc[:, 2:3], gsc[:, 1:2]))
                after(ve.scalar_tensor_tensor(fus[:, :], fus[:, :], gsc[:, 2:3], member[:, :], ALU.mult, ALU.mult))
                for k in range(K):
                    if k % 4 == 0:
                        ve.wait_ge(go_done, k // 4 + 1)
                    ins = ve.tensor_scalar(gF[:, k * P:(k + 1) * P], gnn_out(k), 0.0,
                                           fus[:, k % NG:k % NG + 1], ALU.max, ALU.mult)
                after(ins)
                tell(ve.tensor_reduce(gout[:, :, :], gF.rearrange("p (h g d) -> p h d g", h=HALF, g=NG), AX_X, ALU.add),
                     gout_ready)

            def gnn_add():
                ve.wait_ge(gadd_in, 16 * B)
                ve.wait_ge(x_in[LAST], 16)
                after(ve.tensor_tensor(res[0:NODES, LAST], res[0:NODES, LAST], gadd[:, :, :], ALU.add))

            def norm_of(g, second):
                return [norm[:, 2 * second + g % 2, i, :] for i in range(5)]

            def first_moments(g):
                ve.wait_ge(x_in[g], 16)
                for b in range(B):
                    ins = ve.bn_stats(stats[:, 0, b, :], res[:, g, b, :])
                after(ins)
                mean, var, rstd, tmp, _ = norm_of(g, 0)
                moments(stats[:, 0], mean, var, tmp, sqrt1_in)

            def first_norm(g):
                mean, var, rstd, tmp, _ = norm_of(g, 0)
                ve.wait_ge(sqrt1_out, g + 1)
                newton(rstd, var, tmp)
                if g >= 2:
                    ve.wait_ge(xtT_done, 2 * (g - 1))
                    ve.wait_ge(xn_ready, g - 1)
                for b in range(B):
                    ins = ve.tensor_scalar(xt[:, g % 2, b, :], res[:, g, b, :], mean[:, b:b + 1], rstd[:, b:b + 1],
                                           ALU.subtract, ALU.mult)
                tell(ins, xt_ready)
                for b in range(B):
                    ins = ve.bn_stats(stats[:, 1, b, :], xt[:, g % 2, b, :])
                after(ins)
                mean, var, rstd, tmp, _ = norm_of(g, 1)
                moments(stats[:, 1], mean, var, tmp, sqrt2_in)

            def second_norm(g):
                mean, var, rstd, tmp, shift = norm_of(g, 1)
                ve.wait_ge(sqrt2_out, g + 1)
                newton(rstd, var, tmp)
                after(ve.tensor_scalar(rstd, rstd, float(2 ** SX), None, ALU.mult))
                tell(ve.scalar_tensor_tensor(shift, mean, -1.0, rstd, ALU.mult, ALU.mult), norm2_ready)

            def token_parts(g):
                ve.wait_ge(xn_ready, g + 1)
                after(ve.tensor_copy(hi_part[:, g], xn[:, :, :]))
                tell(ve.tensor_tensor(lo_part[:, g], xn[:, :, :], hi_part[:, g], ALU.subtract), split_x)

            def over(a):
                return a.rearrange("p (t o) -> p t o", o=1).to_broadcast([P, B, E])

            def along(a):
                return a.rearrange("p (o e) -> p o e", o=1).to_broadcast([P, B, E])

            def route(g):
                ve.wait_ge(logit_done, g + 1)
                tell(ve.tensor_tensor(logit[:, :, :], bank[6][:, 0:B * E].rearrange("p (t e) -> p t e", e=E),
                                      along(br_b[:, :]), ALU.add), logit_read)
                for i in range(2):
                    t = top[:, i, g * B:(g + 1) * B]
                    after(ve.tensor_reduce(t, logit[:, :, :], AX_X, ALU.max))
                    after(ve.tensor_tensor(eq[:, :, :], logit[:, :, :], over(t), ALU.is_equal))
                    after(ve.scalar_tensor_tensor(eq[:, :, :], eq[:, :, :], -float(2 * E), along(e_less[:, :]), ALU.mult, ALU.add))
                    after(ve.tensor_reduce(best[:, :], eq[:, :, :], AX_X, ALU.min))
                    after(ve.tensor_tensor(oh[:, g, :, i, :], eq[:, :, :], over(best[:, :]), ALU.is_equal))
                    if i == 0:
                        after(ve.scalar_tensor_tensor(logit[:, :, :], oh[:, g, :, 0, :], -3.0e38, logit[:, :, :], ALU.mult, ALU.add))
                after(ve.tensor_tensor(onehot[:, g], oh[:, g, :, 0, :], oh[:, g, :, 1, :], ALU.add))
                after(ve.tensor_reduce(count[:, :], onehot[:, g].rearrange("p t e -> p e t"), AX_X, ALU.add))
                tell(ve.tensor_tensor(counted[:, g + 1, :], counted[:, g, :], count[:, :], ALU.add), onehot_ready)

            def places(g):
                ve.wait_ge(rank_done, g + 1)
                after(ve.tensor_tensor(place[:, :, :], bank[7][:, 0:B * E].rearrange("p (t e) -> p t e", e=E),
                                       along(e_start[:, :]), ALU.add))
                after(ve.tensor_tensor(chosen[:, :, :, :], oh[:, g],
                                       place[:, :, :].rearrange("p t (o e) -> p t o e", o=1).to_broadcast([P, B, 2, E]), ALU.mult))
                after(ve.tensor_reduce(posf[:, :, :], chosen[:, :, :, :], AX_X, ALU.add))
                tell(ve.tensor_copy(pos[:, g], posf[:, :, :]), pos_ready)

            def weight_maxima():
                ve.wait_ge(folded, 1)
                ve.wait_ge(w2_in, 16 * E)
                after(ve.tensor_tensor(b1T[:, :], bank[0][:, 0:E * HC], cols[:, 0:E * HC], ALU.add))
                ve.tensor_reduce(wmax[:, 0:1], w1f[:, :], AX_X, ALU.max, apply_absolute_value=True)
                ve.tensor_reduce(wmax[:, 1:2], b1T[:, :], AX_X, ALU.max, apply_absolute_value=True)
                tell(ve.tensor_reduce(wmax[:, 2:3], w2f[:, :], AX_X, ALU.max, apply_absolute_value=True), wmax_ready)

            def weight_top():
                ve.wait_ge(wmax_T, 1)
                after(ve.tensor_reduce(wdiag[:, 4:5], bank[1][0:4, 0:P], AX_X, ALU.max))
                tell(ve.tensor_scalar(wdiag[:, 0:4], ident[0:4, 0:4], wdiag[:, 4:5], None, ALU.mult), wdiag_ready)

            def weight_scales():
                ve.wait_ge(wtop_done, 1)
                after(ve.tensor_copy(wtop[:, :], bank[1][:, P:P + 4]))
                after(ve.scalar_tensor_tensor(wtop[:, 1:2], wtop[:, 0:1], float(D), wtop[:, 1:2], ALU.mult, ALU.add))
                after(ve.tensor_scalar(wtop[:, 0:3], wtop[:, 0:3], 1e-30, None, ALU.max))
                after(ve.tensor_scalar(pow2[:, 0:3].bitcast(U32), wtop[:, 0:3].bitcast(U32), 0x7F800000, None, ALU.bitwise_and))
                after(ve.reciprocal(scl[:, 5:8], pow2[:, 0:3]))
                after(ve.tensor_scalar(scl[:, 0:2], scl[:, 5:7], float(2 ** 14), None, ALU.mult))
                after(ve.tensor_scalar(scl[:, 3:4], scl[:, 7:8], float(2 ** 14), None, ALU.mult))
                after(ve.tensor_scalar(scl[:, 2:3], pow2[:, 0:1], 2.0 ** -(14 + SX), None, ALU.mult))
                tell(ve.scalar_tensor_tensor(scl[:, 4:5], pow2[:, 1:2], 2.0 ** -28, pow2[:, 2:3], ALU.mult, ALU.mult), scales_ready)

            def weight_rest():
                for i, (dst, src, s) in enumerate(((w1p, w1f, 0), (w2p, w2f, 3))):
                    ve.wait_ge(whi_ready, i + 1)
                    to = dst[:, :].rearrange("p (n a d) -> p n a d", a=2, d=P)
                    ve.scalar_tensor_tensor(to[:, :, 1, :], src[:, :].rearrange("p (n d) -> p n d", d=P), scl[:, s:s + 1],
                                            to[:, :, 0, :], ALU.mult, ALU.subtract).then_inc(weights_ready, 1)

            def fusion_max():
                ve.wait_ge(gw_in, 16 * (5 + NG))
                after(ve.tensor_reduce(gsc[:, 0:1], fus[:, :], AX_X, ALU.max))
                tell(ve.tensor_scalar(gsc[:, 0:1], gsc[:, 0:1], -1.0, None, ALU.mult), fus_max)

            def take_columns():
                ve.wait_ge(stage_T, 1)
                tell(ve.tensor_copy(cols[:, 0:64], bank[4][:, 0:64]), cols_ready)

            fusion_max()
            ve.wait_ge(ranks_consts, 5)
            for n in range(NS + 3):
                if n == 0:
                    gnn_moments()
                if n == 1:
                    gnn_degrees()
                if 3 <= n:
                    token_parts(n - 3)
                if 2 <= n < NS + 2:
                    route(n - 2)
                if n == 1:
                    gnn_scale()
                    take_columns()
                if n == 2:
                    gnn_transposed()
                if n == 3:
                    gnn_inputs()
                if n == 4:
                    gnn_support()
                if n == NS - 1:
                    gnn_add()
                if 2 <= n < NS + 2:
                    second_norm(n - 2)
                if n == 5:
                    gnn_mix()
                if n == NS:
                    weight_maxima()
                if n == NS + 1:
                    weight_scales()
                if 2 <= n < NS + 2:
                    places(n - 2)
                if n == NS:
                    weight_top()
                if 1 <= n < NS + 1:
                    first_norm(n - 1)
                if n < NS:
                    first_moments(n)

            total, units_f, upto, one_row = (ct[0:1, i, :] for i in range(4))
            ve.wait_ge(filled, 3)
            ve.wait_ge(total_done, 1)
            ve.tensor_tensor(ct_i[0:1, 1, :], bank[2][0:1, 0:E], e_start[0:1, :], ALU.add)
            ve.memset(one_row, 1.0)
            after(ve.tensor_scalar(total, bank[2][0:1, 0:E], float(UNIT - 1), None, ALU.add))
            after(ve.tensor_copy(ct_i[0:1, 0, :], total))
            after(ve.tensor_scalar(ct_i[0:1, 0, :], ct_i[0:1, 0, :], UNIT.bit_length() - 1, None, ALU.logical_shift_right))
            after(ve.tensor_copy(units_f, ct_i[0:1, 0, :]))
            after(ve.tensor_tensor_scan(upto, one_row, units_f, 0.0, ALU.mult, ALU.add))

            def per_unit(a):
                return a.rearrange("o (u e) -> o u e", u=1).to_broadcast([1, NU, E])

            expert, start = ut[0:1, 0, :], ut[0:1, 1, :]
            after(ve.tensor_tensor(cmp[:, :, :], per_unit(upto), unit_no[:, :].rearrange("o (u e) -> o u e", e=1).to_broadcast([1, NU, E]), ALU.is_le))
            after(ve.tensor_reduce(expert, cmp[:, :, :], AX_X, ALU.add))
            after(ve.tensor_tensor(cmp[:, :, :], cmp[:, :, :], per_unit(units_f), ALU.mult))
            after(ve.tensor_reduce(start, cmp[:, :, :], AX_X, ALU.add))
            after(ve.tensor_tensor(start, unit_no[:, :], start, ALU.subtract))
            after(ve.tensor_scalar(start, start, float(UNIT), None, ALU.mult))
            after(ve.scalar_tensor_tensor(start, expert, float(CAP), start, ALU.mult, ALU.add))
            after(ve.tensor_scalar(expert, expert, float(E - 1), None, ALU.min))
            ve.tensor_scalar(unit_row[:, :], start, float(E * CAP), None, ALU.min)
            ve.tensor_scalar(unit_b[:, :], expert, float(HC), None, ALU.mult)
            tell(ve.tensor_scalar(unit_w[:, :], expert, float(2 * H), None, ALU.mult), table_ready)
            weight_rest()
            tell(ve.tensor_tensor(gate[:, 2, :], top[:, 1, :], top[:, 0, :], ALU.subtract), gates_in)
            ve.wait_ge(gates_exp, 1)
            after(ve.tensor_scalar(gate[:, 0, :], gate[:, 2, :], 1.0, None, ALU.add))
            after(ve.reciprocal(gate[:, 0, :], gate[:, 0, :]))
            after(ve.tensor_tensor(gate[:, 1, :], gate[:, 2, :], gate[:, 0, :], ALU.mult))

            def gated(i):
                return gate[:, i, :].rearrange("p (g b o) -> p g b o", b=B, o=1).to_broadcast([P, NS, B, E])

            for i in range(2):
                ins = ve.tensor_tensor(oh[:, :, :, i, :], oh[:, :, :, i, :], gated(i), ALU.mult)
            after(ins)
            after(ve.tensor_tensor(goh[:, :, :, :], oh[:, :, :, 0, :], oh[:, :, :, 1, :], ALU.add))
            after(ve.tensor_scalar(gate[:, 0:2, :], gate[:, 0:2, :], scl[:, 4:5], None, ALU.mult))

            def turn(u, k, it):
                ve.wait_ge(blk_T, u + 1)
                if it is not None or k >= 2:
                    ve.wait_ge(up_done, u - 1)
                ve.tensor_copy(bT[:, k % 2, :], bank[6 + k % 2][:, 0:UNIT].bitcast(F16)).then_inc(bT_ready, 1)

            def second_parts(u, k, it):
                ve.wait_ge(hi_done, u + 1)
                ve.scalar_tensor_tensor(hp[:, k % 3, 1, :], hf[:, k % 2, :], scl[:, 1:2], hp[:, k % 3, 0, :],
                                        ALU.mult, ALU.subtract).then_inc(split_done, 1)

            def evacuate(u, k, it):
                ve.wait_ge(down_done, u + 1)
                two = bank[4 + k % 2][:, :].rearrange("p (a w d) -> p a w d", a=HALVES, w=2)
                ve.tensor_copy(ob[:, k, :, :], two[:, :, 0, :]).then_inc(half_out, 1)
                ve.wait_ge(half_out, u + 1)
                ve.tensor_tensor(ob[:, k, :, :], ob[:, k, :, :], two[:, :, 1, :], ALU.add).then_inc(evacuated, 1)

            def back(u, k, it, lag):
                return u - lag, (k - lag) % UNROLL, it

            turn(0, 0, None)

            def units(u, k, it):
                if not (isinstance(it, int) and k == UNROLL - 1):
                    turn(u + 1, (k + 1) % UNROLL, it if k + 1 < UNROLL else 0)
                if it is not None or k >= 3:
                    evacuate(*back(u, k, it, 3))
                if it is not None or k >= 1:
                    second_parts(*back(u, k, it, 1))

            unit_loop(ve, units)
            second_parts(NU - 1, UNROLL - 1, 0)
            for lag in (3, 2, 1):
                evacuate(NU - lag, UNROLL - lag, 0)

            ve.wait_ge(b2_in, 16 * (P // E))
            for k in range(NB):
                ve.wait_ge(stored[k], 16 * HALVES * NIT)
            tell(ve.tensor_tensor(b2x, b2rep[:, :].rearrange("p (o d) -> p o d", o=1).to_broadcast([P, 2 * B, D]),
                                  delta[:, :].rearrange("p (t o) -> p t o", o=1).to_broadcast([P, 2 * B, D]), ALU.mult), b2x_ready)
            for r in range(NS // 2):
                ve.wait_ge(GT_done, r + 1)
                tell(ve.tensor_copy(GT[:, :], bank[4][:, 0:P]), GT_ready)
                for q in range(4):
                    ve.wait_ge(bias_sum, 4 * r + q + 1)
                    to = res[:, 2 * r + q // 2, (q % 2) * 4:(q % 2) * 4 + 4, :]
                    tell(ve.tensor_tensor(to, to, bank[q][:, :].rearrange("p (t d) -> p t d", d=D), ALU.add), bias_added)
            for g in range(NS):
                ve.wait_ge(y_in[g % YB], 32 * (g // YB + 1))
                for i in range(2):
                    for b in range(B):
                        n = g * B + b
                        ins = ve.scalar_tensor_tensor(res[:, g, b, :], yb[:, g % YB, b, i * D:(i + 1) * D],
                                                      gate[:, i, n:n + 1], res[:, g, b, :], ALU.mult, ALU.add)
                    if i == 0:
                        after(ins)
                ins.then_inc(summed, 1)

        @block.tensor
        def _(pe):
            def gnn_turn():
                pe.wait_ge(gA_ready, 1)
                for k in range(K):
                    mm = pe.transpose(bank[k // 4][:, (k % 4) * P:(k % 4 + 1) * P], gA[:, k * P:(k + 1) * P], ident[:, :])
                    if k % 4 == 3 or k == K - 1:
                        mm.then_inc(gT_done, 1)

            def gnn_first():
                pe.wait_ge(gNT_ready, 3)
                for h in range(HALF):
                    rhs = gNT[:, h * NG * P:(h + 1) * NG * P]
                    pe.matmul(bank[3 + h][:, :], gx[:, h, :], rhs[:, 0:4 * P], start=True, stop=True)
                    pe.matmul(bank[2][:, 256 + h * P:256 + (h + 1) * P], gx[:, h, :], rhs[:, 4 * P:5 * P],
                              start=True, stop=True).then_inc(xa_done, 1)

            def gnn_hidden():
                pe.wait_ge(xaT_ready, 2 * HALF)
                for n in range(NG * GC):
                    g = n // GC
                    mm = pe.matmul(bank[n // 2][:, (n % 2) * 256:(n % 2) * 256 + HALF * P], gW1s[:, n * P:(n + 1) * P],
                                   xaT[:, g * HALF * P:(g + 1) * HALF * P], start=True, stop=True)
                    if n % 2:
                        mm.then_inc(h1_done, 1)

            def gnn_second():
                pe.wait_ge(h1_act, NG * GC)
                for k in range(K):
                    h, g = k // NG, k % NG
                    for c in range(GC):
                        n = (g * GC + c) * HALF + h
                        mm = pe.matmul(bank[k // 4][:, (k % 4) * P:(k % 4 + 1) * P], h1T[:, n * P:(n + 1) * P],
                                       gW2s[:, (g * GC + c) * D:(g * GC + c + 1) * D], start=(c == 0), stop=(c == GC - 1))
                    if k % 4 == 3 or k == K - 1:
                        mm.then_inc(s2_done, 1)

            def gnn_out(k):
                return bank[3 + k // 4][:, (k % 4) * P:(k % 4 + 1) * P] if k < 8 else bank[2][:, 256 + (k - 8) * P:256 + (k - 7) * P]

            def gnn_last():
                pe.wait_ge(s2_ready, 3)
                for k in range(K):
                    pe.matmul(gnn_out(k), gNT[:, k * P:(k + 1) * P], gS2[:, k * P:(k + 1) * P], start=True, stop=False)
                    mm = pe.matmul(gnn_out(k), ones[0:1, :], gb2r[0:1, (k % NG) * D:(k % NG + 1) * D], start=False, stop=True)
                    if k % 4 == 3 or k == K - 1:
                        mm.then_inc(go_done, 1)

            def turn_tokens(g):
                pe.wait_ge(xt_ready, g + 1)
                if g >= 1:
                    pe.wait_ge(xtT_ready, 2 * g)
                for b in range(B):
                    if b == 4:
                        pe.wait_ge(xtT_ready, 2 * g + 1)
                    mm = pe.transpose(bank[5][:, (b % 4) * P:(b % 4 + 1) * P], xt[:, g % 2, b, :], ident[:, :])
                    if b % 4 == 3:
                        mm.then_inc(xtT_done, 1)

            def logits(g):
                pe.wait_ge(xtT_ready, 2 * g + 2)
                if g >= 1:
                    pe.wait_ge(logit_read, g)
                for b in range(B):
                    mm = pe.matmul(bank[6][:, b * E:(b + 1) * E], xtT[:, b * P:(b + 1) * P], wr_sb[:, :],
                                   start=True, stop=True)
                mm.then_inc(logit_done, 1)

            def ranks(g):
                pe.wait_ge(onehot_ready, g + 1)
                pe.matmul(bank[7][:, 0:B * E], tri[:, :], onehot[:, g], start=True, stop=False)
                for b in range(B - 1):
                    n = B - 1 - b
                    pe.matmul(bank[7][:, (b + 1) * E:B * E], ones16[:, :],
                              onehot[:, g, b:b + 1, :].to_broadcast([P, n, E]), start=False, stop=False)
                pe.matmul(bank[7][:, 0:B * E], ones16[:, :],
                          counted[:, g:g + 1, :].to_broadcast([P, B, E]), start=False, stop=True).then_inc(rank_done, 1)

            def folded_bias():
                pe.wait_ge(w1_in, 16)
                pe.wait_ge(cols_ready, 1)
                for n in range(E * HC):
                    e = n // HC
                    mm = pe.matmul(bank[0][:, n:n + 1], w1f[:, n * P:(n + 1) * P], cols[:, 40 + e:41 + e],
                                   start=True, stop=True)
                mm.then_inc(bias_done, 1)

            def weight_top():
                pe.wait_ge(wmax_ready, 1)
                pe.transpose(bank[1][0:4, 0:P], wmax[:, :], ident[:, :]).then_inc(wmax_T, 1)
                pe.wait_ge(wdiag_ready, 1)
                pe.matmul(bank[1][:, P:P + 4], ones[0:4, :], wdiag[:, 0:4], start=True, stop=True).then_inc(wtop_done, 1)

            pe.wait_ge(consts, 5)
            pe.wait_ge(ranks_consts, 5)
            pe.wait_ge(small_in, 16 * 6)
            pe.wait_ge(dve_stage, 1)
            pe.transpose(bank[4][:, 0:P], stage[:, :], ident[:, :]).then_inc(stage_T, 1)
            pe.wait_ge(gw_in, 16 * (5 + NG))
            for n in range(NS + 2):
                if n == 1:
                    gnn_turn()
                if n == 2:
                    gnn_first()
                if 2 <= n:
                    ranks(n - 2)
                if n == 3:
                    gnn_hidden()
                    gnn_second()
                if n == 4:
                    gnn_last()
                if n == 5:
                    folded_bias()
                if n == NS:
                    weight_top()
                if 1 <= n < NS + 1:
                    turn_tokens(n - 1)
                    logits(n - 1)
            pe.matmul(bank[2][:, 0:E], ones16[:, :], counted[:, NS, :], start=True, stop=True).then_inc(total_done, 1)

            pe.wait_ge(table_ready, 1)
            pe.wait_ge(weights_ready, 2)

            def turn_rows(u, k, it):
                pe.wait_ge(blk_in[k], 16 if it is None else 16 * (it + 1))
                if it is not None or k >= 2:
                    pe.wait_ge(bT_ready, u - 1)
                for part in range(2):
                    for a in range(HALVES):
                        w = a * W_ROW + part * D // 2
                        o = (part * HALVES + a) * P // 2
                        mm = pe.transpose(bank[6 + k % 2][:, o:o + P // 2].bitcast(F16),
                                          blk[:, k, w:w + D // 2].bitcast(F16), ident16[:, :])
                mm.then_inc(blk_T, 1)

            def up(u, k, it):
                w = pe.value_load(unit_w[0:1, bass.ds(u, 1)], min_val=0, max_val=(E - 1) * 2 * H)
                pe.wait_ge(bT_ready, u + 1)
                if it is not None or k >= 2:
                    pe.wait_ge(gelu_done, u - 1)
                pe.wait_ge(table_ready, 1)
                for c in range(HC):
                    o = bank[2 * (k % 2) + c // 2][:, (c % 2) * UNIT:(c % 2 + 1) * UNIT]
                    for m, (wa, xa) in enumerate(((0, 0), (0, 1), (1, 0))):
                        mm = pe.matmul(o, w1p[:, bass.ds(w + (2 * c + wa) * P, P)],
                                       bT[:, k % 2, xa * UNIT:(xa + 1) * UNIT], start=(m == 0), stop=(m == 2))
                mm.then_inc(up_done, 1)
                return w

            def down(u, k, it, w):
                if w is None:
                    w = pe.value_load(unit_w[0:1, bass.ds(u, 1)], min_val=0, max_val=(E - 1) * 2 * H)
                pe.wait_ge(split_done, u + 1)
                if it is not None or k >= 2:
                    pe.wait_ge(evacuated, u - 1)
                pe.wait_ge(table_ready, 1)
                for c in range(HC):
                    for a in range(HALVES):
                        o = bank[4 + k % 2]
                        s = slice(c * UNIT + a * P, c * UNIT + (a + 1) * P)

                        def wide():
                            return pe.matmul(o[:, a * UNIT:(a + 1) * UNIT], hp[:, k % 3, 0, s],
                                             w2p[:, bass.ds(w + 2 * c * P, 2 * P)], start=(c == 0 and a == 0), stop=(c == HC - 1 and a == HALVES - 1))

                        def narrow():
                            return pe.matmul(o[:, a * UNIT:a * UNIT + P], hp[:, k % 3, 1, s],
                                             w2p[:, bass.ds(w + 2 * c * P, P)], start=False, stop=False)

                        if c == 0:
                            wide()
                            narrow()
                        else:
                            narrow()
                            mm = wide()
                mm.then_inc(down_done, 1)

            turn_rows(0, 0, None)
            held = {}

            def units(u, k, it):
                if k + 1 < UNROLL:
                    turn_rows(u + 1, k + 1, it)
                elif not isinstance(it, int):
                    turn_rows(u + 1, 0, 1 if it is None else it + 1)
                held[k] = up(u, k, it)
                if it is not None or k >= 2:
                    down(u - 2, (k - 2) % UNROLL, it, held[k - 2] if k >= 2 else None)

            unit_loop(pe, units)
            for lag in (2, 1):
                down(NU - lag, UNROLL - lag, 0, None)

            pe.wait_ge(b2x_ready, 1)
            for r in range(NS // 2):
                if r >= 1:
                    pe.wait_ge(GT_ready, r)
                pe.transpose(bank[4][:, 0:P], goh[:, 2 * r:2 * r + 2].rearrange("p g t e -> p (g t e)"),
                             ident[:, :]).then_inc(GT_done, 1)
                pe.wait_ge(GT_ready, r + 1)
                for q in range(4):
                    if r >= 1:
                        pe.wait_ge(bias_added, 4 * (r - 1) + q + 1)
                    pe.matmul(bank[q][:, :], GT[:, :], b2x[:, 4 * q:4 * q + 4, :], start=True, stop=True
                              ).then_inc(bias_sum, 1)


_INS = ['x', 'adj', 'L0_gnn_W1', 'L0_gnn_b1', 'L0_gnn_W2', 'L0_gnn_b2', 'L0_gnn_fusion_w', 'L0_ffn_Wr',
        'L0_ffn_br', 'L0_ffn_ln_g', 'L0_ffn_ln_b', 'L0_ffn_W1', 'L0_ffn_b1', 'L0_ffn_W2', 'L0_ffn_b2']


def kernel(**inputs):
    import numpy as _np
    import concourse.bacc as _bacc
    from concourse import mybir as _mybir
    from concourse.bass_utils import run_bass_kernel_spmd as _run

    nc = _bacc.Bacc("TRN2", target_bir_lowering=False, num_devices=1)
    arrays = {f"in_{name}_dram": _np.ascontiguousarray(inputs[name]) for name in _INS}
    arrays["group_pairs_dram"], arrays["group_members_dram"] = group_tables()
    args = [nc.dram_tensor(name, a.shape, _mybir.dt.from_np(a.dtype), kind="ExternalInput").ap()
            for name, a in arrays.items()]
    out = nc.dram_tensor("out_0_dram", inputs["x"].shape, _mybir.dt.float32, kind="ExternalOutput").ap()
    build(nc, *args, out)
    r = _run(nc, [arrays], core_ids=[0])
    return r.results[0]["out_0_dram"]
```

```python
from contextlib import ExitStack

import numpy as np

import concourse.bass as bass
import concourse.mybir as mybir

ALU = mybir.AluOpType
ACT = mybir.ActivationFunctionType
F32 = mybir.dt.float32
F16 = mybir.dt.float16
BF16 = mybir.dt.bfloat16
I32 = mybir.dt.int32
U32 = mybir.dt.uint32
AX_X = mybir.AxisListType.X

P = 128
GROUPS = [list(range(25)), [0, 1, 2, 3, 4, 5, 6, 7, 8], [0, 9, 10, 11, 12, 13, 14],
          [6, 7, 8, 12, 13, 14], [3, 4, 5, 9, 10, 11]]
NODES = 25
SLOT = 32
EPS = 1e-5

W_ID = 128
W_ROW = 129
NO_TOKEN = 1 << 20
HALVES = 2
UNIT = HALVES * P
UNROLL = 6
SX = 11
TABLE_MIN = "the table is made of minima with the largest expert"


def group_tables():
    member = np.zeros((P, len(GROUPS)), np.float32)
    for g, nodes in enumerate(GROUPS):
        for j in range(P // SLOT):
            member[[SLOT * j + n for n in nodes], g] = 1.0
    both = member[:, :, None] * member.T[None, :, :]
    return np.ascontiguousarray(both.reshape(P, -1)), member


def units_bound(tokens, experts):
    return (2 * tokens + experts * (UNIT - 1)) // UNIT


def build(nc, x, adj, gW1, gb1, gW2, gb2, fusion, Wr, br, ln_g, ln_b, W1, b1, W2, b2,
          both_in, member_in, out):
    B, S, D = x.shape
    E, _, H = W1.shape
    NG, _, GH = gW1.shape
    assert D == P
    N = B * S
    T = N // P
    HC = H // P
    GC = GH // P
    NU = units_bound(N, E)
    PASSES = NU // UNROLL
    REST = NU % UNROLL
    assert PASSES >= 3 and REST >= 3
    CAP = N + UNIT
    HSPLIT = HC * UNIT // 2
    HALF = B * SLOT // P
    BPH = P // SLOT
    K = NG * HALF
    NS = S // P
    LAST = NS - 1

    def tile_of(g):
        return (g + 1) % NS

    STAGES = NS + 4

    def group(n):
        return n if 0 <= n < LAST else LAST if n == LAST + 2 else None

    x_tiles = x.rearrange("b (j p) d -> j p b d", p=P)
    out_tiles = out.rearrange("b (j p) d -> j p b d", p=P)
    pool = nc.dram_tensor("pool", [E * CAP + UNIT, W_ROW], F32, kind="Internal").ap()
    picked = nc.dram_tensor("picked", [2 * N, D], F32, kind="Internal").ap()
    picked_tiles = picked.rearrange("(b j p two) d -> j p b (two d)", b=B, p=P, two=2)

    with ExitStack() as ctx:
        def sb(name, shape, dt=F32):
            return ctx.enter_context(nc.sbuf_tensor(name, shape, dt))

        def sem(name):
            return ctx.enter_context(nc.semaphore(name))

        bank = [ctx.enter_context(nc.psum_tensor(f"bank{i}", [P, 512], F32)) for i in range(8)]

        res = sb("res", [P, NS, B, D])
        rows = sb("rows", [P, NS, B, W_ROW])
        parts = rows[:, :, :, 0:D].bitcast(F16)
        hi_part, lo_part = parts[:, :, :, 0:D], parts[:, :, :, D:2 * D]
        ids = rows[:, :, :, W_ID:W_ID + 1].bitcast(I32)
        xt = sb("xt", [P, 2, B, D])
        xtT = sb("xtT", [P, B * P])
        assert E * D <= B * P
        b2_all = xtT[:, 0:E * D]
        stats = sb("stats", [P, 2, B, 6])
        norm = sb("norm", [P, 2, 5, 2, B])
        fill = sb("fill", [P, HALVES * W_ROW])

        ident = sb("ident", [P, P])
        ident16 = sb("ident16", [P, P], F16)
        ones = sb("ones", [P, P])
        ones16 = sb("ones16", [P, P], BF16)
        tri = sb("tri", [P, P], BF16)
        e_less = sb("e_less", [P, E])
        e_start = sb("e_start", [P, E])
        unit_no = sb("unit_no", [1, NU])

        stage = sb("stage", [P, P])
        cols = sb("cols", [P, 64])
        w1f = sb("w1f", [P, E * H])
        w2f = sb("w2f", [P, E * H])
        w1p = sb("w1p", [P, E * HC * 2 * P], F16)
        w2p = sb("w2p", [P, E * HC * 2 * P], F16)
        b1T = sb("b1T", [P, E * HC])
        wmax = sb("wmax", [P, 4])
        wtop = sb("wtop", [P, 4])
        wdiag = sb("wdiag", [4, 8])
        pow2 = sb("pow2", [P, 4])
        scl = sb("scl", [P, 8])
        wr_sb = sb("wr_sb", [P, E])
        br_b = sb("br_b", [P, E])

        logit = sb("logit", [P, B, E])
        eq = sb("eq", [P, B, E])
        best = sb("best", [P, B])
        top = sb("top", [P, 2, T])
        oh = sb("oh", [P, NS, B, 2, E])
        onehot = sb("onehot", [P, NS, B, E], BF16)
        count = sb("count", [P, E])
        counted = sb("counted", [P, NS + 1, E], BF16)
        place = sb("place", [P, B, E])
        chosen = sb("chosen", [P, B, 2, E])
        posf = sb("posf", [P, B, 2])
        pos = sb("pos", [P, NS, B, 2], U32)
        gate = sb("gate", [P, 3, T])
        ct = sb("ct", [1, 6, E])
        ct_i = sb("ct_i", [1, 2, E], I32)
        cmp = sb("cmp", [1, NU, E])
        ut = sb("ut", [1, 4, NU])
        unit_row = sb("unit_row", [1, NU], I32)
        unit_w = sb("unit_w", [1, NU], I32)
        unit_b = sb("unit_b", [1, NU], I32)
        unit_d = sb("unit_d", [1, NU], I32)
        gx = sb("gx", [P, HALF, D])
        gsmall = sb("gsmall", [P, 64])
        gmean, gvar, grstd, gtmp = (gsmall[:, 2 * i:2 * i + 2] for i in range(4))
        gdeg, gdinv, gzero, gsafe = (gsmall[:, 10 + 10 * i:20 + 10 * i] for i in range(4))
        gstats = sb("gstats", [P, HALF, 6])
        fus = sb("fus", [P, NG])
        member = sb("member", [P, NG])
        gsc = sb("gsc", [P, 4])
        gb2r = sb("gb2r", [1, NG * D])
        gadd = sb("gadd", [NODES, B, D])

        SHARED = 8716
        shared = sb("shared", [P, SHARED])

        def carver(limit):
            at = [0]

            def take(n):
                at[0] += n
                assert at[0] <= limit
                return shared[:, at[0] - n:at[0]]
            return take

        take = carver(SHARED)
        gW1s = take(NG * GH)
        gW2s = take(NG * GC * D)
        gNT = take(K * P)
        gA = take(K * P)
        xaT = take(K * P)
        h1T = w2p[:, :].bitcast(F32)[:, 0:NG * GC * HALF * P]
        gboth = take(NG * P)
        gZ = take(HALF * P)
        gS2 = gA
        gF = xaT
        gout = take(HALF * D).rearrange("p (h d) -> p h d", h=HALF)
        xn_second = take(B * D).rearrange("p (b d) -> p b d", b=B)
        xn = [sb("xn_first", [P, B, D])[:, :, :], xn_second]

        take = carver(SHARED)
        NB = UNROLL
        blk = take(NB * HALVES * W_ROW).rearrange("p (k w) -> p k w", k=NB)
        bT = take(2 * UNIT).bitcast(F16).rearrange("p (k w) -> p k w", k=2)
        hf = take(2 * HC * UNIT).rearrange("p (k h) -> p k h", k=2)
        hp = take(3 * HC * UNIT).bitcast(F16).rearrange("p (k a h) -> p k a h", k=3, a=2)
        kept = sb("kept", [P, NB, HALVES], U32)
        ob = take(NB * UNIT).rearrange("p (k a d) -> p k a d", k=NB, a=HALVES)

        YB = 4
        take = carver(SHARED)
        yb = take(YB * B * 2 * D).rearrange("p (k b w) -> p k b w", k=YB, b=B)
        x_in = [sem(f"x_in{i}") for i in range(NS)]
        gx_in = sem("gx_in")
        gadj_in = sem("gadj_in")
        gw_in = sem("gw_in")
        router_in = sem("router_in")
        small_in = sem("small_in")
        w1_in = sem("w1_in")
        w2_in = sem("w2_in")
        b2_in = sem("b2_in")
        gadd_in = sem("gadd_in")
        zeroed = sem("zeroed")
        ranks_consts = sem("ranks_consts")
        consts = sem("consts")
        filled = sem("filled")
        v = sem("v")
        fus_max = sem("fus_max")
        fus_exp = sem("fus_exp")
        gsqrt_in = sem("gsqrt_in")
        gsqrt_out = sem("gsqrt_out")
        gA_ready = sem("gA_ready")
        gT_done = sem("gT_done")
        gNT_ready = sem("gNT_ready")
        xa_done = sem("xa_done")
        xaT_ready = sem("xaT_ready")
        h1_done = sem("h1_done")
        h1_act = sem("h1_act")
        s2_done = sem("s2_done")
        s2_ready = sem("s2_ready")
        go_done = sem("go_done")
        gout_ready = sem("gout_ready")
        stage_T = sem("stage_T")
        cols_ready = sem("cols_ready")
        sqrt_in = sem("sqrt_in")
        sqrt_out = sem("sqrt_out")
        norm_ready = sem("norm_ready")
        xt_ready = sem("xt_ready")
        hi_ready = sem("hi_ready")
        xtT_done = sem("xtT_done")
        xtT_ready = sem("xtT_ready")
        logit_done = sem("logit_done")
        logit_read = sem("logit_read")
        xn_ready = sem("xn_ready")
        split_x = sem("split_x")
        onehot_ready = sem("onehot_ready")
        rank_done = sem("rank_done")
        pos_ready = sem("pos_ready")
        ids_ready = sem("ids_ready")
        sent_first = [sem(f"sent_first{i}") for i in range(2)]
        sent_second = sem("sent_second")
        padded = sem("padded")
        total_done = sem("total_done")
        table_ready = sem("table_ready")
        gates_in = sem("gates_in")
        gates_exp = sem("gates_exp")
        bias_done = sem("bias_done")
        folded = sem("folded")
        wmax_ready = sem("wmax_ready")
        wmax_T = sem("wmax_T")
        wdiag_ready = sem("wdiag_ready")
        wtop_done = sem("wtop_done")
        scales_ready = sem("scales_ready")
        whi_ready = sem("whi_ready")
        weights_ready = sem("weights_ready")
        blk_in = [sem(f"blk_in{k}") for k in range(NB)]
        blk_T = [sem(f"blk_T{k}") for k in range(NB)]
        ids_kept = [sem(f"ids_kept{k}") for k in range(NB)]
        bT_ready = [sem(f"bT_ready{k}") for k in range(NB)]
        up_done = [sem(f"up_done{k}") for k in range(NB)]
        gelu_done = [sem(f"gelu_done{k}") for k in range(NB)]
        hi_done = [sem(f"hi_done{k}") for k in range(NB)]
        split_done = [sem(f"split_done{k}") for k in range(NB)]
        down_done = [sem(f"down_done{k}") for k in range(NB)]
        halfway = [sem(f"halfway{k}") for k in range(NB)]
        evacuated = [sem(f"evacuated{k}") for k in range(NB)]
        going = sem("going")
        stored = [sem(f"stored{k}") for k in range(NB)]
        y_in = [sem(f"y_in{k}") for k in range(YB)]
        scaled = sem("scaled")
        summed = sem("summed")
        out_sent = sem("out_sent")

        block = ctx.enter_context(nc.Block())

        def unit_loop(eng, step):
            def steps(i):
                known = {}

                def done(k, lag, by=1, less=0):
                    passes = 1 + (k - lag) // UNROLL
                    if isinstance(i, int):
                        return by * (i + passes) - less if i + passes > 0 else None
                    if (passes, by, less) not in known:
                        known[passes, by, less] = eng.snap((i + passes) * by - less)
                    return known[passes, by, less]

                for k in range(UNROLL if not isinstance(i, int) or i < PASSES else REST):
                    step(i * UNROLL + k, k, done)

            steps(0)
            steps(1)
            with eng.Fori(2, PASSES) as i:
                steps(i)
            steps(PASSES)

        def slot(k, lag):
            return (k - lag) % UNROLL

        def at_end(k, lag, by=1, less=0):
            return by * (PASSES + 1 + (k - lag) // UNROLL) - less

        def all_stored(eng):
            for k in range(UNROLL):
                eng.wait_ge(stored[k], 16 * HALVES * (PASSES + (k < REST)))

        @block.sync
        def _(sp):
            sp.dma_start(res[:, 0], x_tiles[tile_of(0)]).then_inc(x_in[0], 16)
            sp.dma_start(wr_sb[:, :], Wr).then_inc(router_in, 16)
            sp.dma_start(br_b[:, :], br.rearrange("(o e) -> o e", o=1).to_broadcast([P, E])).then_inc(router_in, 16)
            sp.dma_start(res[:, 1], x_tiles[tile_of(1)]).then_inc(x_in[1], 16)
            sp.wait_ge(zeroed, 3)
            sp.dma_start(stage[0:E * HC, :], b1.rearrange("e (c h) -> (e c) h", h=P)).then_inc(small_in, 16)
            sp.dma_start(stage[32:32 + E, :], ln_g).then_inc(small_in, 16)
            sp.dma_start(stage[40:40 + E, :], ln_b).then_inc(small_in, 16)
            sp.dma_start(stage[48:48 + NG * GC, :], gb1.rearrange("g (c h) -> (g c) h", h=P)).then_inc(small_in, 16)
            sp.dma_start(res[:, 2], x_tiles[tile_of(2)]).then_inc(x_in[2], 16)
            for h in range(HALF):
                for j in range(BPH):
                    sp.dma_start(gx[SLOT * j:SLOT * j + NODES, h, :], x[h * BPH + j, 0:NODES, :]).then_inc(gx_in, 16)
            sp.dma_start(gboth, both_in).then_inc(gw_in, 16)
            for b in range(B):
                p0 = SLOT * (b % BPH)
                c0 = (b // BPH) * P + p0
                sp.dma_start(gZ[p0:p0 + NODES, c0:c0 + NODES], adj[b, 0:NODES, 0:NODES]).then_inc(gadj_in, 16)
            sp.dma_start(res[:, 3], x_tiles[tile_of(3)]).then_inc(x_in[3], 16)
            sp.dma_start(fus[:, :], fusion.rearrange("(o g) -> o g", o=1).to_broadcast([P, NG])).then_inc(gw_in, 16)
            sp.dma_start(member[:, :], member_in).then_inc(gw_in, 16)
            sp.dma_start(gW1s.rearrange("p (g h) -> p g h", g=NG), gW1.rearrange("g d h -> d g h")).then_inc(gw_in, 16)
            sp.dma_start(gW2s.rearrange("p (n d) -> p n d", d=D), gW2.rearrange("g (c p) d -> p (g c) d", p=P)).then_inc(gw_in, 16)
            sp.dma_start(gb2r[:, :], gb2.rearrange("(o g) d -> o (g d)", o=1)).then_inc(gw_in, 16)
            for g in range(4, NS):
                sp.dma_start(res[:, g], x_tiles[tile_of(g)]).then_inc(x_in[g], 16)
            sp.dma_start(w1f[:, :].rearrange("p (e h) -> p e h", e=E), W1.rearrange("e d h -> d e h")).then_inc(w1_in, 16)
            for e in range(0, E, 2):
                sp.dma_start(w2f[:, e * H:(e + 2) * H].rearrange("p (n d) -> p n d", d=D),
                             W2[e:e + 2].rearrange("e (c p) d -> p (e c) d", p=P)).then_inc(w2_in, 16)
            sp.wait_ge(filled, 2)
            sp.dma_start(pool[E * CAP:E * CAP + UNIT, :].rearrange("(p a) w -> p (a w)", p=P), fill[:, :]
                         ).then_inc(padded, 16)
            sp.wait_ge(gout_ready, 1)
            for b in range(B):
                p0 = SLOT * (b % BPH)
                sp.dma_start(gadd[:, b, :], gout[p0:p0 + NODES, b // BPH, :]).then_inc(gadd_in, 16)
            sp.wait_ge(table_ready, 1)
            for e in range(E):
                row = sp.value_load(ct_i[0:1, 1, e:e + 1], min_val=0, max_val=E * CAP)
                sp.dma_start(pool[bass.ds(row, UNIT), :].rearrange("(p a) w -> p (a w)", p=P), fill[:, :]
                             ).then_inc(padded, 16)
            sp.dma_start(b2_all[:, :], b2.rearrange("(o e) d -> o (e d)", o=1).to_broadcast([P, E * D])).then_inc(b2_in, 16)
            for i in range(2):
                sp.wait_ge(sent_first[i], 16 * T // 2)
            sp.wait_ge(sent_second, 16 * T)
            sp.wait_ge(padded, 16 * (E + 1))

            def load(u, k, done):
                row = sp.value_load(unit_row[0:1, bass.ds(u, 1)], min_val=0, max_val=E * CAP)
                if done(k, UNROLL) is not None:
                    sp.wait_ge(blk_T[k], done(k, UNROLL))
                    sp.wait_ge(ids_kept[k], done(k, UNROLL))
                sp.dma_start(blk[:, k, :], pool[bass.ds(row, UNIT), :].rearrange("(p a) w -> p (a w)", p=P)
                             ).then_inc(blk_in[k], 16)

            unit_loop(sp, load)

            all_stored(sp)
            half = [slice(h * B // 2, (h + 1) * B // 2) for h in range(2)]

            def fetch(g, h):
                sp.dma_start(yb[:, g % YB, half[h], :], picked_tiles[tile_of(g)][:, half[h], :]
                             ).then_inc(y_in[g % YB] if h else x_in[g], 16)

            for g in range(YB):
                for h in range(2):
                    fetch(g, h)
            for g in range(NS):
                for h in range(2):
                    sp.wait_ge(summed, 2 * g + h + 1)
                    sp.dma_start(out_tiles[tile_of(g)][:, half[h], :], res[:, g, half[h], :]).then_inc(out_sent, 16)
                    if g + YB < NS:
                        fetch(g + YB, h)
            sp.wait_ge(out_sent, 32 * NS)

        @block.gpsimd
        def _(po):
            po.memset(ones16[:, :], 1.0).then_inc(ranks_consts, 1)
            po.memset(tri[:, :], 1.0).then_inc(ranks_consts, 1)
            po.memset(ident[:, :], 0.0).then_inc(consts, 1)
            po.memset(ident16[:, :], 0.0).then_inc(consts, 1)
            po.iota(e_less[:, :], [[1, E]], base=-E, channel_multiplier=0,
                    allow_small_or_imprecise_dtypes=True).then_inc(ranks_consts, 1)
            po.iota(e_start[:, :], [[CAP, E]], base=0, channel_multiplier=0,
                    allow_small_or_imprecise_dtypes=True).then_inc(ranks_consts, 1)
            po.wait_ge(ranks_consts, 4)
            po.affine_select(out=tri[:, :], in_=tri[:, :], compare_op=ALU.is_gt, fill=0.0, base=0,
                             pattern=[[1, P]], channel_multiplier=-1).then_inc(ranks_consts, 1)
            po.wait_ge(consts, 2)
            for m in (ident, ident16):
                po.affine_select(out=m[:, :], in_=m[:, :], compare_op=ALU.not_equal, fill=1.0, base=0,
                                 pattern=[[-1, P]], channel_multiplier=1).then_inc(consts, 1)
            po.memset(fill[:, :], 0.0).then_inc(filled, 1)
            po.wait_ge(filled, 1)
            po.iota(fill[:, :].rearrange("p (a w) -> p a w", a=HALVES)[:, :, W_ID:W_ID + 1].bitcast(I32), [[0, HALVES]],
                    base=NO_TOKEN, channel_multiplier=0).then_inc(filled, 1)
            po.iota(unit_no[:, :], [[1, NU]], base=0, channel_multiplier=0,
                    allow_small_or_imprecise_dtypes=True).then_inc(filled, 1)

            def number(g, which):
                po.iota(ids[:, g], [[2 * S, B]], base=2 * P * tile_of(g) + which, channel_multiplier=2
                        ).then_inc(ids_ready, 1)
                po.wait_ge(ids_ready, made[0] + 1)
                made[0] += 1

            made = [0]

            def send(g, which, tiles=range(B)):
                for b in tiles:
                    po.indirect_dma_start(pool, bass.IndirectOffsetOnAxis(ap=pos[:, g, b, which:which + 1], axis=0),
                                          rows[:, g, b, :], None, bounds_check=E * CAP - 1,
                                          oob_is_err=False).then_inc(sent_second if which else sent_first[g % 2], 16)

            for g in range(NS):
                number(g, 0)

            def send_first(g):
                po.wait_ge(pos_ready, g + 1)
                po.wait_ge(split_x, g + 1)
                send(g, 0)

            def send_second(g):
                po.wait_ge(sent_first[g % 2], 16 * B * (g // 2 + 1))
                number(g, 1)
                send(g, 1, range(B - OVER))

            OVER = 2
            send_first(0)
            for g in range(1, NS):
                send_second(g - 1)
                send_first(g)
                send(g - 1, 1, range(B - OVER, B))
            send_second(LAST)
            send(LAST, 1, range(B - OVER, B))

            def keep(u, k, done):
                po.wait_ge(blk_in[k], done(k, 0, 16))
                if done(k, UNROLL) is not None:
                    po.wait_ge(stored[k], done(k, UNROLL, 16 * HALVES))
                po.sem_inc(going, 1)
                po.tensor_copy(kept[:, k, :], blk[:, k, :].rearrange("p (a w) -> p a w", a=HALVES)[:, :, W_ID].bitcast(U32)
                               ).then_inc(ids_kept[k], 1)

            def store(k, lag, done):
                n = slot(k, lag)
                po.wait_ge(evacuated[n], done(k, lag))
                po.wait_ge(ids_kept[n], done(k, lag))
                po.sem_inc(going, 1)
                for a in range(HALVES):
                    po.indirect_dma_start(picked, bass.IndirectOffsetOnAxis(ap=kept[:, n, a:a + 1], axis=0),
                                          ob[:, n, a, :], None, bounds_check=2 * N - 1,
                                          oob_is_err=False).then_inc(stored[n], 16)

            def units(u, k, done):
                keep(u, k, done)
                if done(k, 3) is not None:
                    store(k, 3, done)

            unit_loop(po, units)
            for lag in (3, 2, 1):
                store(REST, lag, at_end)

        @block.scalar
        def _(act):
            def fusion_exp():
                act.wait_ge(fus_max, 1)
                act.activation(fus[:, :], fus[:, :], ACT.Exp, bias=gsc[:, 0:1], accum_out=gsc[:, 1:2]).then_inc(fus_exp, 1)

            def gnn_root(n):
                act.wait_ge(gsqrt_in, n + 1)
                if n == 0:
                    act.activation(grstd, gtmp, ACT.Sqrt).then_inc(gsqrt_out, 1)
                else:
                    act.activation(gdinv, gsafe, ACT.Sqrt).then_inc(gsqrt_out, 1)

            def gnn_hidden():
                act.wait_ge(cols_ready, 1)
                for n in range(NG * GC):
                    if n % 2 == 0:
                        act.wait_ge(h1_done, n // 2 + 1)
                    act.activation(h1T[:, n * HALF * P:(n + 1) * HALF * P],
                                   bank[n // 2][:, (n % 2) * 256:(n % 2) * 256 + HALF * P],
                                   ACT.Relu, bias=cols[:, 48 + n:49 + n]).then_inc(h1_act, 1)

            def root(n):
                act.wait_ge(sqrt_in, n + 1)
                act.activation(norm[:, n % 2, 2], norm[:, n % 2, 3], ACT.Sqrt).then_inc(sqrt_out, 1)

            def first_norm(g, n):
                act.wait_ge(norm_ready, n)
                for b in range(B):
                    act.activation(xt[:, g % 2, b, :], res[:, g, b, :], ACT.Identity,
                                   bias=norm[:, (n - 1) % 2, 4, 0, b:b + 1], scale=norm[:, (n - 1) % 2, 2, 0, b:b + 1]
                                   ).then_inc(xt_ready, 1)

            def copy_tokens(g, h):
                act.wait_ge(xtT_done, 2 * g + h + 1)
                if g >= 1 and h == 0:
                    act.wait_ge(logit_done, g)
                act.activation(xtT[:, h * 512:(h + 1) * 512], bank[5][:, :], ACT.Copy).then_inc(xtT_ready, 1)

            def second_norm(g, n):
                act.wait_ge(norm_ready, n)
                if g >= 2:
                    act.wait_ge(split_x, g - 1)
                for b in range(B):
                    ins = act.activation(xn[g % 2][:, b, :], xt[:, g % 2, b, :], ACT.Identity,
                                         bias=norm[:, (n - 1) % 2, 4, 1, b:b + 1], scale=norm[:, (n - 1) % 2, 2, 1, b:b + 1])
                ins.then_inc(xn_ready, 1)

            def first_part(g):
                act.wait_ge(xn_ready, g + 1)
                act.activation(hi_part[:, g], xn[g % 2], ACT.Copy, scale=float(2 ** SX)).then_inc(hi_ready, 1)

            def fold():
                act.wait_ge(bias_done, 2)
                for e in range(E):
                    ins = act.activation(w1f[:, e * H:(e + 1) * H], w1f[:, e * H:(e + 1) * H], ACT.Copy,
                                         scale=cols[:, 32 + e:33 + e])
                ins.then_inc(folded, 1)

            def weight_parts():
                act.wait_ge(scales_ready, 1)
                for dst, src, s in ((w1p, w1f, 0), (w2p, w2f, 3)):
                    to = dst[:, :].rearrange("p (n a d) -> p n a d", a=2, d=P)[:, :, 0, :]
                    act.activation(to, src[:, :].rearrange("p (n d) -> p n d", d=P), ACT.Copy,
                                   scale=scl[:, s:s + 1]).then_inc(whi_ready, 1)

            for n in range(STAGES):
                if group(n - 1) is not None:
                    first_norm(group(n - 1), n)
                if n == 7:
                    gnn_hidden()
                if n <= 2:
                    root(n)
                if group(n - 2) is not None:
                    second_norm(group(n - 2), n)
                if n == 3:
                    root(n)
                if group(n - 1) is not None:
                    copy_tokens(group(n - 1), 0)
                if group(n - 2) is not None:
                    first_part(group(n - 2))
                if group(n - 1) is not None:
                    copy_tokens(group(n - 1), 1)
                if 3 < n < STAGES - 1:
                    root(n)
                if n == 1:
                    gnn_root(0)
                if n == 4:
                    gnn_root(1)
                if n == 4:
                    fusion_exp()
                if n == 5:
                    fold()
            act.wait_ge(gates_in, 1)
            act.activation(gate[:, 2, :], gate[:, 2, :], ACT.Exp).then_inc(gates_exp, 1)
            weight_parts()
            act.activation(gsc[:, 3:4], gsc[:, 0:1], ACT.Gelu)
            act.wait_ge(table_ready, 1)

            def gelus(u, k, done):
                first = nc.values_load(unit_b[0:1, bass.ds(u, 1)], engines=[mybir.EngineType.Activation],
                                       min_val=0, max_val=(E - 1) * HC, skip_runtime_bounds_check_because=TABLE_MIN)
                if done(k, 2) is not None:
                    act.wait_ge(split_done[slot(k, 2)], done(k, 2))
                act.wait_ge(up_done[k], done(k, 0))
                for c in range(HC):
                    ins = act.activation(hf[:, k % 2, c * UNIT:(c + 1) * UNIT],
                                         bank[2 * (k % 2) + c // 2][:, (c % 2) * UNIT:(c % 2 + 1) * UNIT], ACT.Gelu,
                                         bias=b1T[:, bass.ds(first + c, 1)], scale=scl[:, 2:3])
                ins.then_inc(gelu_done[k], 1)
                if done(k, 3) is not None:
                    act.wait_ge(down_done[slot(k, 3)], done(k, 3))
                act.wait_ge(gelu_done[k], done(k, 0))
                act.activation(hp[:, k % 3, 0, 0:HSPLIT], hf[:, k % 2, 0:HSPLIT], ACT.Copy, scale=scl[:, 1:2]
                               ).then_inc(hi_done[k], 1)

            unit_loop(act, gelus)

            for g in range(NS):
                for h in range(2):
                    if h:
                        act.wait_ge(y_in[g % YB], 16 * (g // YB + 1))
                    else:
                        act.wait_ge(x_in[g], 32)
                    for b in range(h * B // 2, (h + 1) * B // 2):
                        n = g * B + b
                        y = yb[:, g % YB, b, D:2 * D]
                        ins = act.activation(y, y, ACT.Copy, scale=gate[:, 1, n:n + 1])
                    ins.then_inc(scaled, 1)

        @block.vector
        def _(ve):
            made = [0]

            def after(ins, meanwhile=None):
                made[0] += 1
                ins.then_inc(v, 1)
                count = made[0]
                if meanwhile is not None:
                    meanwhile()
                ve.wait_ge(v, count)

            told = {}

            def tell(ins, s):
                told[s.name] = told.get(s.name, 0) + 1
                ins.then_inc(s, 1)
                ve.wait_ge(s, told[s.name])

            def newton(r, y, tmp):
                after(ve.tensor_tensor(tmp, r, r, ALU.mult))
                after(ve.scalar_tensor_tensor(tmp, tmp, -0.5, y, ALU.mult, ALU.mult))
                after(ve.scalar_tensor_tensor(r, tmp, 1.5, r, ALU.add, ALU.mult))

            def moments(st, mean_, var_, tmp_, need_sqrt):
                ve.tensor_tensor(mean_, st(1), st(4), ALU.add)
                ve.tensor_tensor(tmp_, st(1), st(4), ALU.subtract)
                after(ve.tensor_tensor(var_, st(2), st(5), ALU.add))
                ve.tensor_scalar(mean_, mean_, 0.5, None, ALU.mult)
                ve.tensor_scalar(var_, var_, 1.0 / D, EPS, ALU.mult, ALU.add)
                after(ve.scalar_tensor_tensor(tmp_, tmp_, 0.25, tmp_, ALU.mult, ALU.mult))
                after(ve.tensor_tensor(var_, var_, tmp_, ALU.add))
                tell(ve.reciprocal(tmp_, var_), need_sqrt)

            ve.memset(stage[:, :], 0.0).then_inc(zeroed, 1)
            ve.memset(gx[:, :, :], 0.0).then_inc(zeroed, 1)
            ve.memset(gZ, 0.0).then_inc(zeroed, 1)
            ve.memset(ones[:, :], 1.0)
            ve.memset(stats[:, :, :, :], 0.0)
            ve.memset(wmax[:, :], 0.0)
            after(ve.memset(counted[:, 0, :], 0.0))

            def spread(a, n):
                return a.rearrange("p (k o) -> p k o", o=1).to_broadcast([P, n, P])

            gA3 = gA.rearrange("p (k m) -> p k m", k=K)

            def gnn_moments():
                ve.wait_ge(gx_in, 16 * B)
                for h in range(HALF):
                    ins = ve.bn_stats(gstats[:, h, :], gx[:, h, :])
                after(ins)
                moments(lambda i: gstats[:, :, i], gmean, gvar, gtmp, gsqrt_in)

            def gnn_degrees():
                ve.wait_ge(gadj_in, 16 * B)
                ve.wait_ge(consts, 4)
                ve.wait_ge(gw_in, 16 * 6)
                gA4 = gA.rearrange("p (h g m) -> p h g m", h=HALF, g=NG)
                for h in range(HALF):
                    ins = ve.tensor_tensor(gZ[:, h * P:(h + 1) * P], gZ[:, h * P:(h + 1) * P], ident[:, :], ALU.add)
                after(ins)
                for h in range(HALF):
                    ins = ve.tensor_tensor(gA4[:, h], gZ[:, h * P:(h + 1) * P].rearrange("p (o m) -> p o m", o=1).to_broadcast([P, NG, P]),
                                           gboth.rearrange("p (g m) -> p g m", g=NG), ALU.mult)
                after(ins)
                after(ve.tensor_reduce(gdeg, gA3, AX_X, ALU.add))
                after(ve.tensor_scalar(gzero, gdeg, 0.0, None, ALU.is_equal))
                after(ve.tensor_tensor(gdeg, gdeg, gzero, ALU.add))
                tell(ve.reciprocal(gsafe, gdeg), gsqrt_in)
                ve.wait_ge(gsqrt_out, 1)
                newton(grstd, gvar, gtmp)
                for h in range(HALF):
                    ins = ve.tensor_scalar(gx[:, h, :], gx[:, h, :], gmean[:, h:h + 1], grstd[:, h:h + 1],
                                           ALU.subtract, ALU.mult)
                after(ins)

            def gnn_scale():
                ve.wait_ge(gsqrt_out, 2)
                newton(gdinv, gdeg, gsafe)
                after(ve.tensor_scalar(gzero, gzero, -1.0, 1.0, ALU.mult, ALU.add))
                after(ve.tensor_tensor(gdinv, gdinv, gzero, ALU.mult))
                tell(ve.tensor_tensor(gA3, gA3, spread(gdinv, K), ALU.mult), gA_ready)

            def gnn_transposed():
                gN3 = gNT.rearrange("p (k m) -> p k m", k=K)
                for q in range(3):
                    n = min(4, K - 4 * q)
                    ve.wait_ge(gT_done, q + 1)
                    ve.tensor_tensor(gN3[:, 4 * q:4 * q + n], bank[q][:, 0:n * P].rearrange("p (k m) -> p k m", k=n),
                                     spread(gdinv[:, 4 * q:4 * q + n], n), ALU.mult).then_inc(gNT_ready, 1)

            def gnn_inputs():
                xa4 = xaT.rearrange("p (g h m) -> p g h m", g=NG, h=HALF)
                for h in range(HALF):
                    ve.wait_ge(xa_done, h + 1)
                    ve.tensor_copy(xa4[:, 0:4, h, :], bank[3 + h][:, :].rearrange("p (g m) -> p g m", g=4)).then_inc(xaT_ready, 1)
                for h in range(HALF):
                    ve.tensor_copy(xa4[:, 4, h, :], bank[2][:, 256 + h * P:256 + (h + 1) * P]).then_inc(xaT_ready, 1)

            def gnn_support():
                for q in range(3):
                    n = min(4, K - 4 * q)
                    ve.wait_ge(s2_done, q + 1)
                    ve.tensor_copy(gS2[:, 4 * q * P:(4 * q + n) * P], bank[q][:, 0:n * P]).then_inc(s2_ready, 1)

            def gnn_out(k):
                return bank[3 + k // 4][:, (k % 4) * P:(k % 4 + 1) * P] if k < 8 else bank[2][:, 256 + (k - 8) * P:256 + (k - 7) * P]

            def gnn_mix():
                ve.wait_ge(fus_exp, 1)
                after(ve.reciprocal(gsc[:, 2:3], gsc[:, 1:2]))
                after(ve.scalar_tensor_tensor(fus[:, :], fus[:, :], gsc[:, 2:3], member[:, :], ALU.mult, ALU.mult))
                for k in range(K):
                    if k % 4 == 0:
                        ve.wait_ge(go_done, k // 4 + 1)
                    ins = ve.tensor_scalar(gF[:, k * P:(k + 1) * P], gnn_out(k), 0.0,
                                           fus[:, k % NG:k % NG + 1], ALU.max, ALU.mult)
                after(ins)
                tell(ve.tensor_reduce(gout[:, :, :], gF.rearrange("p (h g d) -> p h d g", h=HALF, g=NG), AX_X, ALU.add),
                     gout_ready)

            def gnn_add():
                ve.wait_ge(gadd_in, 16 * B)
                ve.wait_ge(x_in[LAST], 16)
                after(ve.tensor_tensor(res[0:NODES, LAST], res[0:NODES, LAST], gadd[:, :, :], ALU.add))

            def stats_first(g, b):
                if b == 0:
                    ve.wait_ge(x_in[g], 16)
                return ve.bn_stats(stats[:, 0, b, :], res[:, g, b, :])

            def stats_second(g, b):
                ve.wait_ge(xt_ready, B * g + b + 1)
                return ve.bn_stats(stats[:, 1, b, :], xt[:, g % 2, b, :])

            def both_moments(n):
                mean, var, _, tmp = (norm[:, n % 2, i] for i in range(4))
                moments(lambda i: stats[:, :, :, i], mean, var, tmp, sqrt_in)

            def both_norms(n):
                mean, var, rstd, tmp, shift = (norm[:, n % 2, i] for i in range(5))
                ve.wait_ge(sqrt_out, n + 1)
                newton(rstd, var, tmp)
                tell(ve.scalar_tensor_tensor(shift, mean, -1.0, rstd, ALU.mult, ALU.mult), norm_ready)

            def second_part(g):
                ve.wait_ge(hi_ready, g + 1)
                tell(ve.scalar_tensor_tensor(lo_part[:, g], xn[g % 2], float(2 ** SX), hi_part[:, g], ALU.mult, ALU.subtract), split_x)

            def over(a):
                return a.rearrange("p (t o) -> p t o", o=1).to_broadcast([P, B, E])

            def along(a):
                return a.rearrange("p (o e) -> p o e", o=1).to_broadcast([P, B, E])

            def route(g, stat):
                ve.wait_ge(logit_done, g + 1)
                tell(ve.tensor_tensor(logit[:, :, :], bank[6][:, 0:B * E].rearrange("p (t e) -> p t e", e=E),
                                      along(br_b[:, :]), ALU.add), logit_read)
                for i in range(2):
                    t = top[:, i, g * B:(g + 1) * B]
                    after(ve.tensor_reduce(t, logit[:, :, :], AX_X, ALU.max), stat)
                    after(ve.tensor_tensor(eq[:, :, :], logit[:, :, :], over(t), ALU.is_equal), stat)
                    after(ve.scalar_tensor_tensor(eq[:, :, :], eq[:, :, :], -float(2 * E), along(e_less[:, :]), ALU.mult, ALU.add), stat)
                    after(ve.tensor_reduce(best[:, :], eq[:, :, :], AX_X, ALU.min), stat)
                    after(ve.tensor_tensor(oh[:, g, :, i, :], eq[:, :, :], over(best[:, :]), ALU.is_equal), stat)
                    if i == 0:
                        after(ve.scalar_tensor_tensor(logit[:, :, :], oh[:, g, :, 0, :], -3.0e38, logit[:, :, :], ALU.mult, ALU.add), stat)
                after(ve.tensor_tensor(onehot[:, g], oh[:, g, :, 0, :], oh[:, g, :, 1, :], ALU.add), stat)
                after(ve.tensor_reduce(count[:, :], onehot[:, g].rearrange("p t e -> p e t"), AX_X, ALU.add), stat)
                tell(ve.tensor_tensor(counted[:, g + 1, :], counted[:, g, :], count[:, :], ALU.add), onehot_ready)

            def places(g):
                ve.wait_ge(rank_done, g + 1)
                after(ve.tensor_tensor(place[:, :, :], bank[7][:, 0:B * E].rearrange("p (t e) -> p t e", e=E),
                                       along(e_start[:, :]), ALU.add))
                after(ve.tensor_tensor(chosen[:, :, :, :], oh[:, g],
                                       place[:, :, :].rearrange("p t (o e) -> p t o e", o=1).to_broadcast([P, B, 2, E]), ALU.mult))
                after(ve.tensor_reduce(posf[:, :, :], chosen[:, :, :, :], AX_X, ALU.add))
                tell(ve.tensor_copy(pos[:, g], posf[:, :, :]), pos_ready)

            def hidden_bias():
                ve.wait_ge(bias_done, 2)
                after(ve.tensor_tensor(b1T[:, :], bank[4][:, 0:E * HC], cols[:, 0:E * HC], ALU.add))

            def weight_maxima():
                ve.wait_ge(folded, 1)
                ve.wait_ge(w2_in, 16 * E // 2)
                ve.tensor_reduce(wmax[:, 0:1], w1f[:, :], AX_X, ALU.max, apply_absolute_value=True)
                ve.tensor_reduce(wmax[:, 1:2], b1T[:, :], AX_X, ALU.max, apply_absolute_value=True)
                tell(ve.tensor_reduce(wmax[:, 2:3], w2f[:, :], AX_X, ALU.max, apply_absolute_value=True), wmax_ready)

            def weight_top():
                ve.wait_ge(wmax_T, 1)
                after(ve.tensor_reduce(wdiag[:, 4:5], bank[1][0:4, 0:P], AX_X, ALU.max))
                tell(ve.tensor_scalar(wdiag[:, 0:4], ident[0:4, 0:4], wdiag[:, 4:5], None, ALU.mult), wdiag_ready)

            def weight_scales():
                ve.wait_ge(wtop_done, 1)
                after(ve.tensor_copy(wtop[:, :], bank[1][:, P:P + 4]))
                after(ve.scalar_tensor_tensor(wtop[:, 1:2], wtop[:, 0:1], float(D), wtop[:, 1:2], ALU.mult, ALU.add))
                after(ve.tensor_scalar(wtop[:, 0:3], wtop[:, 0:3], 1e-30, None, ALU.max))
                after(ve.tensor_scalar(pow2[:, 0:3].bitcast(U32), wtop[:, 0:3].bitcast(U32), 0x7F800000, None, ALU.bitwise_and))
                after(ve.reciprocal(scl[:, 5:8], pow2[:, 0:3]))
                after(ve.tensor_scalar(scl[:, 0:2], scl[:, 5:7], float(2 ** 14), None, ALU.mult))
                after(ve.tensor_scalar(scl[:, 3:4], scl[:, 7:8], float(2 ** 14), None, ALU.mult))
                after(ve.tensor_scalar(scl[:, 2:3], pow2[:, 0:1], 2.0 ** -(14 + SX), None, ALU.mult))
                tell(ve.scalar_tensor_tensor(scl[:, 4:5], pow2[:, 1:2], 2.0 ** -28, pow2[:, 2:3], ALU.mult, ALU.mult), scales_ready)

            def weight_rest():
                for i, (dst, src, s) in enumerate(((w1p, w1f, 0), (w2p, w2f, 3))):
                    ve.wait_ge(whi_ready, i + 1)
                    to = dst[:, :].rearrange("p (n a d) -> p n a d", a=2, d=P)
                    ve.scalar_tensor_tensor(to[:, :, 1, :], src[:, :].rearrange("p (n d) -> p n d", d=P), scl[:, s:s + 1],
                                            to[:, :, 0, :], ALU.mult, ALU.subtract).then_inc(weights_ready, 1)

            def fusion_max():
                ve.wait_ge(gw_in, 16 * 6)
                after(ve.tensor_reduce(gsc[:, 0:1], fus[:, :], AX_X, ALU.max))
                tell(ve.tensor_scalar(gsc[:, 0:1], gsc[:, 0:1], -1.0, None, ALU.mult), fus_max)

            def take_columns():
                ve.wait_ge(stage_T, 1)
                tell(ve.tensor_copy(cols[:, 0:64], bank[4][:, 0:64]), cols_ready)

            ve.wait_ge(ranks_consts, 5)
            for n in range(STAGES):
                if n >= 1:
                    both_norms(n - 1)
                if n == LAST + 2:
                    route(group(n - 3), None)
                    second_part(group(n - 3))
                    places(group(n - 3))
                    gnn_add()
                first, second = group(n), group(n - 1)
                left = [(stats_first, first, b) for b in range(B if first is not None else 0)]
                left += [(stats_second, second, b) for b in range(B if second is not None else 0)]

                def stat():
                    if left:
                        f, g, b = left.pop(0)
                        return f(g, b)

                done = n in (3, LAST + 2) or group(n - 3) is None
                if not done:
                    route(group(n - 3), stat)
                ins = None
                while left:
                    ins = stat()
                if ins is not None:
                    after(ins)
                if n < STAGES - 1:
                    both_moments(n)
                if n == 1:
                    gnn_moments()
                if n == 6:
                    gnn_inputs()
                if n == LAST + 1:
                    gnn_support()
                if n == 2:
                    ve.wait_ge(router_in, 32)
                    route(0, None)
                    second_part(0)
                    places(0)
                if not done:
                    second_part(group(n - 3))
                    if n == LAST + 1:
                        weight_maxima()
                    places(group(n - 3))
                if n == 3:
                    take_columns()
                if n == 4:
                    fusion_max()
                if n == 4:
                    gnn_degrees()
                if n == 5:
                    gnn_scale()
                    hidden_bias()
                    gnn_transposed()
                if n == LAST + 1:
                    gnn_mix()
            route(LAST, None)
            second_part(LAST)
            places(LAST)

            total, units_f, upto, one_row = (ct[0:1, i, :] for i in range(4))
            ve.wait_ge(filled, 3)
            ve.wait_ge(total_done, 1)
            ve.tensor_tensor(ct_i[0:1, 1, :], bank[2][0:1, 0:E], e_start[0:1, :], ALU.add)
            ve.memset(one_row, 1.0)
            after(ve.tensor_scalar(total, bank[2][0:1, 0:E], float(UNIT - 1), None, ALU.add))
            after(ve.tensor_copy(ct_i[0:1, 0, :], total))
            after(ve.tensor_scalar(ct_i[0:1, 0, :], ct_i[0:1, 0, :], UNIT.bit_length() - 1, None, ALU.logical_shift_right))
            after(ve.tensor_copy(units_f, ct_i[0:1, 0, :]))
            after(ve.tensor_tensor_scan(upto, one_row, units_f, 0.0, ALU.mult, ALU.add))

            def per_unit(a):
                return a.rearrange("o (u e) -> o u e", u=1).to_broadcast([1, NU, E])

            expert, start = ut[0:1, 0, :], ut[0:1, 1, :]
            after(ve.tensor_tensor(cmp[:, :, :], per_unit(upto), unit_no[:, :].rearrange("o (u e) -> o u e", e=1).to_broadcast([1, NU, E]), ALU.is_le))
            after(ve.tensor_reduce(expert, cmp[:, :, :], AX_X, ALU.add))
            after(ve.tensor_tensor(cmp[:, :, :], cmp[:, :, :], per_unit(units_f), ALU.mult))
            after(ve.tensor_reduce(start, cmp[:, :, :], AX_X, ALU.add))
            after(ve.tensor_tensor(start, unit_no[:, :], start, ALU.subtract))
            after(ve.tensor_scalar(start, start, float(UNIT), None, ALU.mult))
            after(ve.scalar_tensor_tensor(start, expert, float(CAP), start, ALU.mult, ALU.add))
            after(ve.tensor_scalar(expert, expert, float(E - 1), None, ALU.min))
            ve.tensor_scalar(unit_row[:, :], start, float(E * CAP), None, ALU.min)
            ve.tensor_scalar(unit_b[:, :], expert, float(HC), None, ALU.mult)
            ve.tensor_scalar(unit_d[:, :], expert, float(D), None, ALU.mult)
            tell(ve.tensor_scalar(unit_w[:, :], expert, float(2 * H), None, ALU.mult), table_ready)
            weight_top()
            tell(ve.tensor_tensor(gate[:, 2, :], top[:, 1, :], top[:, 0, :], ALU.subtract), gates_in)
            weight_scales()
            ve.wait_ge(gates_exp, 1)
            after(ve.tensor_scalar(gate[:, 0, :], gate[:, 2, :], 1.0, None, ALU.add))
            after(ve.reciprocal(gate[:, 0, :], gate[:, 0, :]))
            after(ve.tensor_tensor(gate[:, 1, :], gate[:, 2, :], gate[:, 0, :], ALU.mult))
            weight_rest()

            def turn(k, done):
                n = slot(k, -1)
                if done(k, 1) is not None:
                    ve.wait_ge(up_done[slot(k, 1)], done(k, 1))
                ve.wait_ge(blk_T[n], done(k, -1))
                ve.tensor_copy(bT[:, n % 2, :], bank[6 + n % 2][:, 0:UNIT].bitcast(F16)).then_inc(bT_ready[n], 1)

            def first_parts(k, lag, done):
                n = slot(k, lag)
                if done(k, lag + 3) is not None:
                    ve.wait_ge(down_done[slot(k, lag + 3)], done(k, lag + 3))
                ve.wait_ge(gelu_done[n], done(k, lag))
                ve.tensor_scalar(hp[:, n % 3, 0, HSPLIT:], hf[:, n % 2, HSPLIT:], scl[:, 1:2], None, ALU.mult
                                 ).then_inc(halfway[n], 1)

            def second_parts(k, lag, done):
                n = slot(k, lag)
                ve.wait_ge(hi_done[n], done(k, lag))
                ve.wait_ge(halfway[n], done(k, lag, 2, 1))
                ve.scalar_tensor_tensor(hp[:, n % 3, 1, :], hf[:, n % 2, :], scl[:, 1:2], hp[:, n % 3, 0, :],
                                        ALU.mult, ALU.subtract).then_inc(split_done[n], 1)

            def output(n):
                two = bank[4 + n % 2][:, :].rearrange("p (a w d) -> p a w d", a=HALVES, w=2)
                return two[:, :, 0, :], two[:, :, 1, :], ob[:, n, :, :]

            def output_first(u, k, lag, done):
                n = slot(k, lag)
                at = nc.values_load(unit_d[0:1, bass.ds(u - lag, 1)], engines=[mybir.EngineType.DVE], min_val=0,
                                    max_val=(E - 1) * D, skip_runtime_bounds_check_because=TABLE_MIN)
                if done(k, lag + UNROLL) is not None:
                    ve.wait_ge(stored[n], done(k, lag + UNROLL, 16 * HALVES))
                ve.wait_ge(down_done[n], done(k, lag))
                first, _, to = output(n)
                bias = b2_all[:, bass.ds(at, D)].rearrange("p (a d) -> p a d", a=1).to_broadcast([P, HALVES, D])
                ve.scalar_tensor_tensor(to, first, scl[:, 4:5], bias, ALU.mult, ALU.add).then_inc(halfway[n], 1)

            def output_second(k, lag, done):
                n = slot(k, lag)
                ve.wait_ge(halfway[n], done(k, lag, 2))
                _, second, to = output(n)
                ve.scalar_tensor_tensor(to, second, scl[:, 4:5], to, ALU.mult, ALU.add).then_inc(evacuated[n], 1)

            ve.wait_ge(b2_in, 16)
            ve.wait_ge(blk_T[0], 1)
            ve.tensor_copy(bT[:, 0, :], bank[6][:, 0:UNIT].bitcast(F16)).then_inc(bT_ready[0], 1)

            def units(u, k, done):
                if done(k, 3) is not None:
                    output_first(u, k, 3, done)
                if not (isinstance(u, int) and u == NU - 1):
                    turn(k, done)
                if done(k, 1) is not None:
                    first_parts(k, 1, done)
                if done(k, 3) is not None:
                    output_second(k, 3, done)
                if done(k, 1) is not None:
                    second_parts(k, 1, done)

            unit_loop(ve, units)

            for lag in (3, 2, 1):
                output_first(NU, REST, lag, at_end)
                if lag == 3:
                    first_parts(REST, 1, at_end)
                output_second(REST, lag, at_end)
                if lag == 3:
                    second_parts(REST, 1, at_end)

            for g in range(NS):
                for h in range(2):
                    if h:
                        ve.wait_ge(y_in[g % YB], 16 * (g // YB + 1))
                    else:
                        ve.wait_ge(x_in[g], 32)
                    for b in range(h * B // 2, (h + 1) * B // 2):
                        n = g * B + b
                        ins = ve.scalar_tensor_tensor(res[:, g, b, :], yb[:, g % YB, b, 0:D],
                                                      gate[:, 0, n:n + 1], res[:, g, b, :], ALU.mult, ALU.add)
                    after(ins)
                    ve.wait_ge(scaled, 2 * g + h + 1)
                    to = res[:, g, h * B // 2:(h + 1) * B // 2, :]
                    ve.tensor_tensor(to, to, yb[:, g % YB, h * B // 2:(h + 1) * B // 2, D:2 * D], ALU.add).then_inc(summed, 1)

        @block.tensor
        def _(pe):
            def gnn_turn():
                pe.wait_ge(gA_ready, 1)
                for k in range(K):
                    mm = pe.transpose(bank[k // 4][:, (k % 4) * P:(k % 4 + 1) * P], gA[:, k * P:(k + 1) * P], ident[:, :])
                    if k % 4 == 3 or k == K - 1:
                        mm.then_inc(gT_done, 1)

            def gnn_first():
                pe.wait_ge(gNT_ready, 3)
                for h in range(HALF):
                    rhs = gNT[:, h * NG * P:(h + 1) * NG * P]
                    pe.matmul(bank[3 + h][:, :], gx[:, h, :], rhs[:, 0:4 * P], start=True, stop=True)
                    pe.matmul(bank[2][:, 256 + h * P:256 + (h + 1) * P], gx[:, h, :], rhs[:, 4 * P:5 * P],
                              start=True, stop=True).then_inc(xa_done, 1)

            def gnn_hidden():
                pe.wait_ge(xaT_ready, 2 * HALF)
                for n in range(NG * GC):
                    g = n // GC
                    mm = pe.matmul(bank[n // 2][:, (n % 2) * 256:(n % 2) * 256 + HALF * P], gW1s[:, n * P:(n + 1) * P],
                                   xaT[:, g * HALF * P:(g + 1) * HALF * P], start=True, stop=True)
                    if n % 2:
                        mm.then_inc(h1_done, 1)

            def gnn_second():
                pe.wait_ge(h1_act, NG * GC)
                for k in range(K):
                    h, g = k // NG, k % NG
                    for c in range(GC):
                        n = (g * GC + c) * HALF + h
                        mm = pe.matmul(bank[k // 4][:, (k % 4) * P:(k % 4 + 1) * P], h1T[:, n * P:(n + 1) * P],
                                       gW2s[:, (g * GC + c) * D:(g * GC + c + 1) * D], start=(c == 0), stop=(c == GC - 1))
                    if k % 4 == 3 or k == K - 1:
                        mm.then_inc(s2_done, 1)

            def gnn_out(k):
                return bank[3 + k // 4][:, (k % 4) * P:(k % 4 + 1) * P] if k < 8 else bank[2][:, 256 + (k - 8) * P:256 + (k - 7) * P]

            def gnn_last():
                pe.wait_ge(s2_ready, 3)
                for k in range(K):
                    pe.matmul(gnn_out(k), gNT[:, k * P:(k + 1) * P], gS2[:, k * P:(k + 1) * P], start=True, stop=False)
                    mm = pe.matmul(gnn_out(k), ones[0:1, :], gb2r[0:1, (k % NG) * D:(k % NG + 1) * D], start=False, stop=True)
                    if k % 4 == 3 or k == K - 1:
                        mm.then_inc(go_done, 1)

            def turn_tokens(g, h):
                if 2 * g + h > 0:
                    pe.wait_ge(xtT_ready, 2 * g + h)
                for b in range(h * B // 2, (h + 1) * B // 2):
                    pe.wait_ge(xt_ready, B * g + b + 1)
                    mm = pe.transpose(bank[5][:, (b % 4) * P:(b % 4 + 1) * P], xt[:, g % 2, b, :], ident[:, :])
                mm.then_inc(xtT_done, 1)

            def logits(g):
                pe.wait_ge(xtT_ready, 2 * g + 2)
                if g >= 1:
                    pe.wait_ge(logit_read, g)
                for b in range(B):
                    mm = pe.matmul(bank[6][:, b * E:(b + 1) * E], xtT[:, b * P:(b + 1) * P], wr_sb[:, :],
                                   start=True, stop=True)
                mm.then_inc(logit_done, 1)

            def ranks(g):
                pe.wait_ge(onehot_ready, g + 1)
                pe.matmul(bank[7][:, 0:B * E], tri[:, :], onehot[:, g], start=True, stop=False)
                for b in range(B - 1):
                    n = B - 1 - b
                    pe.matmul(bank[7][:, (b + 1) * E:B * E], ones16[:, :],
                              onehot[:, g, b:b + 1, :].to_broadcast([P, n, E]), start=False, stop=False)
                pe.matmul(bank[7][:, 0:B * E], ones16[:, :],
                          counted[:, g:g + 1, :].to_broadcast([P, B, E]), start=False, stop=True).then_inc(rank_done, 1)

            def folded_bias(experts):
                for n in range(experts[0] * HC, (experts[-1] + 1) * HC):
                    e = n // HC
                    mm = pe.matmul(bank[4][:, n:n + 1], w1f[:, n * P:(n + 1) * P], cols[:, 40 + e:41 + e],
                                   start=True, stop=True)
                mm.then_inc(bias_done, 1)

            def weight_top():
                pe.wait_ge(wmax_ready, 1)
                pe.transpose(bank[1][0:4, 0:P], wmax[:, :], ident[:, :]).then_inc(wmax_T, 1)
                pe.wait_ge(wdiag_ready, 1)
                pe.matmul(bank[1][:, P:P + 4], ones[0:4, :], wdiag[:, 0:4], start=True, stop=True).then_inc(wtop_done, 1)

            pe.wait_ge(consts, 4)
            pe.wait_ge(ranks_consts, 5)
            pe.wait_ge(router_in, 32)
            for n in range(STAGES):
                if n == 6:
                    gnn_first()
                if group(n - 2) is not None:
                    logits(group(n - 2))
                if group(n - 1) is not None:
                    turn_tokens(group(n - 1), 0)
                if n != 3 and group(n - 3) is not None:
                    ranks(group(n - 3))
                if group(n - 1) is not None:
                    turn_tokens(group(n - 1), 1)
                if n == 2:
                    ranks(0)
                    pe.wait_ge(small_in, 16 * 4)
                    pe.wait_ge(zeroed, 3)
                    pe.transpose(bank[4][:, 0:P], stage[:, :], ident[:, :]).then_inc(stage_T, 1)
                if n == 3:
                    pe.wait_ge(w1_in, 16)
                    pe.wait_ge(cols_ready, 1)
                    folded_bias(range(E // 4))
                if n == 4:
                    folded_bias(range(E // 4, E))
                if n == 5:
                    gnn_turn()
                if n == 6:
                    pe.wait_ge(gw_in, 16 * 6)
                    gnn_hidden()
                if n == 7:
                    gnn_second()
                    gnn_last()
            ranks(LAST)
            pe.matmul(bank[2][:, 0:E], ones16[:, :], counted[:, NS, :], start=True, stop=True).then_inc(total_done, 1)
            weight_top()

            pe.wait_ge(table_ready, 1)
            pe.wait_ge(weights_ready, 2)

            def turn_rows(n, loaded):
                pe.wait_ge(blk_in[n], loaded)
                for part in range(2):
                    for a in range(HALVES):
                        w = a * W_ROW + part * D // 2
                        o = (part * HALVES + a) * P // 2
                        mm = pe.transpose(bank[6 + n % 2][:, o:o + P // 2].bitcast(F16),
                                          blk[:, n, w:w + D // 2].bitcast(F16), ident16[:, :])
                mm.then_inc(blk_T[n], 1)

            def where(u):
                return nc.values_load(unit_w[0:1, bass.ds(u, 1)], engines=[mybir.EngineType.PE], min_val=0,
                                      max_val=(E - 1) * 2 * H, skip_runtime_bounds_check_because=TABLE_MIN)

            def up(u, k, done, w, then=None):
                if done(k, 2) is not None:
                    pe.wait_ge(gelu_done[slot(k, 2)], done(k, 2))
                pe.wait_ge(bT_ready[k], done(k, 0))
                for c in range(HC):
                    if c == 2 and then is not None:
                        held[then[0]] = where(then[1])
                    o = bank[2 * (k % 2) + c // 2][:, (c % 2) * UNIT:(c % 2 + 1) * UNIT]
                    for m, (wa, xa) in enumerate(((0, 0), (0, 1), (1, 0))):
                        mm = pe.matmul(o, w1p[:, bass.ds(w + (2 * c + wa) * P, P)],
                                       bT[:, k % 2, xa * UNIT:(xa + 1) * UNIT], start=(m == 0), stop=(m == 2))
                mm.then_inc(up_done[k], 1)

            def down(k, lag, done, w, then=None):
                n = slot(k, lag)
                pe.wait_ge(split_done[n], done(k, lag))
                o = bank[4 + n % 2]
                for c in range(HC):
                    if c == 2 and then is not None:
                        held[then[0]] = where(then[1])
                    for a in range(HALVES):
                        s = slice(c * UNIT + a * P, c * UNIT + (a + 1) * P)

                        def wide():
                            return pe.matmul(o[:, a * UNIT:(a + 1) * UNIT], hp[:, n % 3, 0, s],
                                             w2p[:, bass.ds(w + 2 * c * P, 2 * P)], start=(c == 0 and a == 0),
                                             stop=(c == HC - 1 and a == HALVES - 1))

                        def narrow():
                            return pe.matmul(o[:, a * UNIT:a * UNIT + P], hp[:, n % 3, 1, s],
                                             w2p[:, bass.ds(w + 2 * c * P, P)], start=False, stop=False)

                        if c == 0:
                            wide()
                            narrow()
                        else:
                            narrow()
                            mm = wide()
                mm.then_inc(down_done[n], 1)

            turn_rows(0, 16)
            held = {}

            def units(u, k, done):
                if not (isinstance(u, int) and u == NU - 1):
                    turn_rows(slot(k, -1), done(k, -1, 16))
                if k == 0:
                    held[0] = where(u)
                    up(u, k, done, held[0], None if done(k, 2) is None else (-2, u - 2))
                else:
                    up(u, k, done, held[k], (-1, u - 2) if k == 1 and done(k, 2) is not None else None)
                ahead = (k + 1, u + 1) if k + 1 < UNROLL and not (isinstance(u, int) and u == NU - 1) else None
                if done(k, 2) is not None:
                    down(k, 2, done, held[k - 2], ahead)
                elif ahead:
                    held[k + 1] = where(u + 1)

            unit_loop(pe, units)
            for lag in (2, 1):
                down(REST, lag, at_end, held[REST - lag])


_INS = ['x', 'adj', 'L0_gnn_W1', 'L0_gnn_b1', 'L0_gnn_W2', 'L0_gnn_b2', 'L0_gnn_fusion_w', 'L0_ffn_Wr',
        'L0_ffn_br', 'L0_ffn_ln_g', 'L0_ffn_ln_b', 'L0_ffn_W1', 'L0_ffn_b1', 'L0_ffn_W2', 'L0_ffn_b2']


def kernel(**inputs):
    import numpy as _np
    import concourse.bacc as _bacc
    from concourse import mybir as _mybir
    from concourse.bass_utils import run_bass_kernel_spmd as _run

    nc = _bacc.Bacc("TRN2", target_bir_lowering=False, num_devices=1)
    arrays = {f"in_{name}_dram": _np.ascontiguousarray(inputs[name]) for name in _INS}
    arrays["group_pairs_dram"], arrays["group_members_dram"] = group_tables()
    args = [nc.dram_tensor(name, a.shape, _mybir.dt.from_np(a.dtype), kind="ExternalInput").ap()
            for name, a in arrays.items()]
    out = nc.dram_tensor("out_0_dram", inputs["x"].shape, _mybir.dt.float32, kind="ExternalOutput").ap()
    build(nc, *args, out)
    r = _run(nc, [arrays], core_ids=[0])
    return r.results[0]["out_0_dram"]
```
